# Optimizing a Trainium2 kernel written in Bass

```python
import numpy as np
import jax
import jax.numpy as jnp

def _softmax(x, axis=-1):
    return jax.nn.softmax(x, axis=axis)

def _gelu(x):
    return jax.nn.gelu(x, approximate=True)

def _silu(x):
    return jax.nn.silu(x)

def _sigmoid(x):
    return jax.nn.sigmoid(x)

def _layernorm(x, axis=-1, eps=1e-05):
    m = jnp.mean(x, axis=axis, keepdims=True)
    v = jnp.var(x, axis=axis, keepdims=True)
    return (x - m) / jnp.sqrt(v + eps)

def _scatter_add(tgt, idx, src, axis=0):
    return tgt.at[idx].add(src)

def _segment_sum(src, seg, n):
    return jax.ops.segment_sum(src, seg, n)
kernel_name = 'mk_flamingo_gated_d1_seqx_r4_ffe0e3'

def setup_inputs(seed: int=0):
    np.random.seed(seed)
    _w = jnp.asarray

    def _rec_inputs():
        import jax
        import jax.numpy as jnp
        _rk = jax.random.key(seed)
        x = -0.0005207 + 1.001 * jax.random.normal(jax.random.fold_in(_rk, 1), (16, 112, 512), jnp.float32)
        _lenS = 112 - jax.random.randint(jax.random.fold_in(_rk, 7), (16,), 0, max(1, 112 // 4) + 1, jnp.int32)
        _lenS2 = 375 - jax.random.randint(jax.random.fold_in(_rk, 8), (16,), 0, max(1, 375 // 4) + 1, jnp.int32)
        _ctx_2048P = jax.random.normal(jax.random.fold_in(_rk, 12), (16, 16, 512), jnp.float32)
        _ctx_2048c = jax.random.dirichlet(jax.random.fold_in(_rk, 512), 0.3 * jnp.ones((16,), jnp.float32), (16, 375))
        _ctx_2048t = jnp.einsum('bsk,bkd->bsd', _ctx_2048c, _ctx_2048P)
        _ctx_2048t = _ctx_2048t * jax.lax.rsqrt(jnp.mean(jnp.square(_ctx_2048t)) + 1e-12) * 0.953939
        ctx_2048 = -5.72187e-05 + 0.999849 * (_ctx_2048t + 0.3 * jax.random.normal(jax.random.fold_in(_rk, 612), (16, 375, 512), jnp.float32))
        _validS = jnp.arange(112)[None, :] < _lenS[:, None]
        _validS2 = jnp.arange(375)[None, :] < _lenS2[:, None]
        _causal = jnp.tril(jnp.ones((112, 112), dtype=bool))
        mask_BxSx4224_bf0 = jnp.logical_not(jnp.ones((16, 112, 1056), dtype=bool))
        _g = jax.random.normal(jax.random.fold_in(_rk, 9001), (2, 1), jnp.float32)
        _g = jnp.sign(_g) * jnp.maximum(jnp.abs(_g), 1.0) + (_g == 0) * 1.0
        g_xattn = _g[0]
        g_ffn = _g[1]
        return (x, ctx_2048, mask_BxSx4224_bf0, g_xattn, g_ffn)
    x, ctx_2048, mask_BxSx4224_bf0, g_xattn, g_ffn = _rec_inputs()

    def _L0_xattn_setup():
        import jax, jax.numpy as jnp
        import numpy as np
        import math
        DIM = 512
        B, Q_LEN, KV_LEN = (8, 128, 1024)
        key = jax.random.key(seed)
        ks = jax.random.split(key, 8)
        x = jax.random.normal(ks[0], (B, Q_LEN, DIM), dtype=jnp.float32)
        mask = jnp.zeros((B, Q_LEN, KV_LEN + Q_LEN), dtype=bool)
        k_cache = jax.random.normal(ks[1], (B, KV_LEN, DIM), dtype=jnp.float32)
        v_cache = jax.random.normal(ks[2], (B, KV_LEN, DIM), dtype=jnp.float32)
        scale = 1.0 / math.sqrt(DIM)
        wq = jax.random.normal(ks[3], (DIM, DIM), dtype=jnp.float32) * scale
        wk = jax.random.normal(ks[4], (DIM, DIM), dtype=jnp.float32) * scale
        wv = jax.random.normal(ks[5], (DIM, DIM), dtype=jnp.float32) * scale
        wo = jax.random.normal(ks[6], (DIM, DIM), dtype=jnp.float32) * scale
        return {'x': x, 'mask': mask, 'k_cache': k_cache, 'v_cache': v_cache, 'wq': wq, 'wk': wk, 'wv': wv, 'wo': wo}
    _L0_xattn_all = _L0_xattn_setup()
    _L0_xattn_in = {k: v for k, v in _L0_xattn_all.items() if k in ('wq', 'wk', 'wv', 'wo')}
    del _L0_xattn_all

    def _L0_ffn_setup():
        import jax, jax.numpy as jnp
        import numpy as np
        EPS = 1e-05

        def act_quant(x):
            scale = 127.0 / jnp.clip(jnp.max(jnp.abs(x), axis=-1, keepdims=True), EPS)
            return jnp.clip(jnp.round(x * scale), -128.0, 127.0) / scale

        def weight_quant(w):
            scale = 1.0 / jnp.clip(jnp.mean(jnp.abs(w)), EPS)
            return jnp.clip(jnp.round(w * scale), -1.0, 1.0) / scale

        def bitlinear(x, w):
            return jnp.einsum('bsd,hd->bsh', act_quant(x), weight_quant(w))
        key = jax.random.key(seed)
        k0, k1, k2, k3 = jax.random.split(key, 4)
        d_model, hidden_dim = (512, 1408)
        B, S = (4, 512)
        x = jax.random.normal(k0, (B, S, d_model), dtype=jnp.float32)
        std = 0.02
        w1 = jax.random.normal(k1, (hidden_dim, d_model), dtype=jnp.float32) * std
        w2 = jax.random.normal(k2, (d_model, hidden_dim), dtype=jnp.float32) * std
        w3 = jax.random.normal(k3, (hidden_dim, d_model), dtype=jnp.float32) * std
        return {'x': x, 'w1': w1, 'w2': w2, 'w3': w3}
    _L0_ffn_all = _L0_ffn_setup()
    _L0_ffn_in = {k: v for k, v in _L0_ffn_all.items() if k in ('w1', 'w2', 'w3')}
    del _L0_ffn_all
    return {'x': x, 'ctx_2048': ctx_2048, 'mask_BxSx4224_bf0': mask_BxSx4224_bf0, 'g_xattn': g_xattn, 'g_ffn': g_ffn, 'L0_xattn_wq': _L0_xattn_in['wq'], 'L0_xattn_wk': _L0_xattn_in['wk'], 'L0_xattn_wv': _L0_xattn_in['wv'], 'L0_xattn_wo': _L0_xattn_in['wo'], 'L0_ffn_w1': _L0_ffn_in['w1'], 'L0_ffn_w2': _L0_ffn_in['w2'], 'L0_ffn_w3': _L0_ffn_in['w3']}

def reference(x, ctx_2048, mask_BxSx4224_bf0, g_xattn, g_ffn, L0_xattn_wq, L0_xattn_wk, L0_xattn_wv, L0_xattn_wo, L0_ffn_w1, L0_ffn_w2, L0_ffn_w3):
    import jax
    import jax.numpy as jnp

    def _L0_xattn_ref(x, mask, k_cache, v_cache, wq, wk, wv, wo):
        import jax, jax.numpy as jnp
        import numpy as np
        import math
        DIM = 512
        B, Q_LEN, KV_LEN = (8, 128, 1024)
        q = jnp.einsum('bsd,ed->bse', x, wq)
        k_new = jnp.einsum('bsd,ed->bse', x, wk)
        v_new = jnp.einsum('bsd,ed->bse', x, wv)
        k = jnp.concatenate([k_cache, k_new], axis=1)
        v = jnp.concatenate([v_cache, v_new], axis=1)
        scale = 1.0 / math.sqrt(q.shape[-1])
        scores = jnp.einsum('bqd,bkd->bqk', q, k) * scale
        attn = jax.nn.softmax(scores, axis=-1)
        out = jnp.einsum('bqk,bkd->bqd', attn, v)
        return jnp.einsum('bqd,ed->bqe', out, wo)

    def _L0_ffn_ref(x, w1, w2, w3):
        import jax, jax.numpy as jnp
        import numpy as np
        EPS = 1e-05

        def act_quant(x):
            scale = 127.0 / jnp.clip(jnp.max(jnp.abs(x), axis=-1, keepdims=True), EPS)
            return jnp.clip(jnp.round(x * scale), -128.0, 127.0) / scale

        def weight_quant(w):
            scale = 1.0 / jnp.clip(jnp.mean(jnp.abs(w)), EPS)
            return jnp.clip(jnp.round(w * scale), -1.0, 1.0) / scale

        def bitlinear(x, w):
            return jnp.einsum('bsd,hd->bsh', act_quant(x), weight_quant(w))
        h = jax.nn.silu(bitlinear(x, w1)) * bitlinear(x, w3)
        return bitlinear(h, w2)
    x = x + jnp.tanh(g_xattn[0]) * _L0_xattn_ref(_layernorm(x, axis=-1), mask_BxSx4224_bf0, ctx_2048, ctx_2048, L0_xattn_wq, L0_xattn_wk, L0_xattn_wv, L0_xattn_wo)
    x = x + jnp.tanh(g_ffn[0]) * _L0_ffn_ref(_layernorm(x, axis=-1), L0_ffn_w1, L0_ffn_w2, L0_ffn_w3)
    return x

_drawn_inputs = setup_inputs


def setup_inputs(seed=0):
    import zlib

    import numpy as np

    out = dict(_drawn_inputs(seed))
    spreads = {}
    factors = {}
    for name, (base, spread) in spreads.items():
        noise = np.random.default_rng([zlib.crc32(name.encode()), seed]).standard_normal(out[name].shape)
        drawn = base * np.exp(spread * noise) if base else spread * noise
        out[name] = jnp.asarray(drawn.astype(out[name].dtype))
    for name, factor in factors.items():
        out[name] = (out[name] * factor).astype(out[name].dtype)
    return out
```

```python
from contextlib import ExitStack

import numpy as np

import concourse.bass as bass
from concourse import mybir

B, TQ, D = 16, 112, 512
KC = 375
F = 1408
P = 128
DC = D // P
FC = F // P
CK = KC // 3
KEYS = KC + TQ
KPAD = KEYS + 1
PPAD = 4 * CK
TOK = B * TQ
NT = TOK // P
GROUPS = B // 2
PAIRS = NT // 2
EPS = 1e-5
SCALE = float(D) ** -0.5
MAGIC = 12582912.0
WCH = 12
NW = float(F * D)
HCH = [(0, 512), (512, 512), (1024, 384)]


def flamingo_kernel(nc, x, ctxT, ctx, g_xattn, g_ffn, wqT, wkT, wvT, woT, wffn, out, o_dram):
    fp32 = mybir.dt.float32
    f32r = mybir.dt.float32r
    bf16 = mybir.dt.bfloat16
    ALU = mybir.AluOpType
    ACT = mybir.ActivationFunctionType
    AX = mybir.AxisListType.X

    x_b = x.rearrange("(n t) d -> n t d", t=TQ)
    o_b = o_dram.rearrange("(n t) d -> n t d", t=TQ)
    x_t = x.rearrange("(n p) d -> n p d", p=P)
    o_t = o_dram.rearrange("(n p) d -> n p d", p=P)
    y_t = out.rearrange("(n p) d -> n p d", p=P)

    keep = ExitStack()
    with keep:
        def sb(name, shape, dt, stack=keep):
            return stack.enter_context(nc.sbuf_tensor(name, shape, dt))

        def sem(name):
            return keep.enter_context(nc.semaphore(name))

        def sems(name, n=2):
            return [sem(f"{name}{i}") for i in range(n)]

        banks = [keep.enter_context(nc.psum_tensor(f"bank{i}", [P, 512], fp32)) for i in range(8)]

        WQ = sb("ffn_ternary", [P, WCH, F], bf16)
        w2q = WQ[:, 8:12, :].rearrange("p a f -> p (a f)").rearrange("p (c n) -> p c n", n=D)
        wbuf = sb("ffn_raw", [P, 2, F], fp32)
        ident = sb("ident", [P, P], fp32)
        identb = sb("identb", [P, P], bf16)
        ones = sb("ones", [P, P], fp32)
        magic = sb("magic", [P, 2], fp32)
        epsc = sb("epsc", [P, 1], fp32)
        gin = sb("gin", [1, 2], fp32)
        gates = sb("gates", [P, 2], fp32)
        wabs = sb("wabs", [P, WCH], fp32)
        wabs3 = sb("wabs3", [P, 3], fp32)
        wmean = sb("wmean", [P, 3], fp32)
        wscale = sb("wscale", [P, 3], fp32)
        wscur = sb("wscur", [P, 1], fp32)
        bn = sb("bn", [TQ, 2, 6], fp32)
        mv = sb("mv", [TQ, 2, 2], fp32)
        std = sb("std", [TQ, 2], fp32)
        rstd = sb("rstd", [TQ, 2], fp32)
        rowmax = sb("rowmax", [TQ, 2], fp32)
        expbias = sb("expbias", [TQ, 2], fp32)
        rowsum = sb("rowsum", [TQ, 2], fp32)
        rowinv = sb("rowinv", [TQ, 2], fp32)

        half1 = ExitStack()
        wsp = [[sb(f"{w}_{s}", [P, DC, D], f32r, half1) for s in ("hi", "lo")] for w in ("wq", "wk", "wv")]
        vv = [sb(f"v_{s}", [P, 2, 4, D], f32r, half1) for s in ("hi", "lo")]
        kT = [sb(f"kT_{s}", [P, 2, DC, KPAD], f32r, half1) for s in ("hi", "lo")]
        kraw = sb("kraw", [P, DC, KC], fp32, half1)
        vraw = sb("vraw", [CK, 3, D], fp32, half1)
        xT = [sb(f"xT_{s}", [P, DC, 2 * TQ], f32r, half1) for s in ("hi", "lo")]
        qT = [sb(f"qT_{s}", [P, DC, 2 * TQ], f32r, half1) for s in ("hi", "lo")]
        xb = sb("xb", [TQ, 2, D], fp32, half1)
        prob = sb("prob", [TQ, 2, PPAD], fp32, half1)
        pT = [sb(f"pT_{s}", [CK, 2, 4 * TQ], f32r, half1) for s in ("hi", "lo")]
        ob = sb("ob", [TQ, 2, D], fp32, half1)
        half1.close()
        start = ExitStack()
        for w in ("wq", "wk", "wv"):
            for s in ("hi", "lo"):
                sb(f"skip_{w}_{s}", [P, DC, D], f32r, start)
        wraw = sb("wraw", [P, 3, DC, D], fp32, start)
        start.close()

        half2 = ExitStack()
        wo = [sb(f"wo_{s}", [P, DC, D], f32r, half2) for s in ("hi", "lo")]
        x1 = sb("x1", [P, NT, D], fp32, half2)
        ot = sb("ot", [P, 2, D], fp32, half2)
        xt = sb("xt", [P, 2, D], fp32, half2)
        oT = [sb(f"oT_{s}", [P, 2, DC, P], f32r, half2) for s in ("hi", "lo")]
        bn2 = sb("bn2", [P, NT * 6], fp32, half2)
        mv2 = sb("mv2", [P, NT, 2], fp32, half2)
        std2 = sb("std2", [P, NT], fp32, half2)
        rstd2 = sb("rstd2", [P, NT], fp32, half2)
        nmean2 = sb("nmean2", [P, NT], fp32, half2)
        wdq = sb("wdq", [P, 3], fp32, half2)
        xc = sb("xc", [P, 2, D], fp32, half2)
        xq = sb("xq", [P, 2, D], bf16, half2)
        xqT = sb("xqT", [P, 2, DC, P], bf16, half2)
        hid = sb("hid", [P, 2, F], fp32, half2)
        hq = sb("hq", [P, 2, F], bf16, half2)
        hqT = sb("hqT", [P, 2, FC, P], bf16, half2)
        yb = sb("yb", [P, 2, D], fp32, half2)
        col = {n: sb(n, [P, 2], fp32, half2) for n in ("xamax", "xclip", "xinv", "xmul", "hamax", "hclip", "hinv", "hmul", "ydq")}
        xdq = sb("xdq", [P, 2, 2], fp32, half2)
        half2.close()

        consts = sem("consts")
        g_in, tanh_mm, gates_ok = sem("g_in"), sem("tanh_mm"), sem("gates_ok")
        pw_in, pw_hi, pw_lo = sems("pw_in", 3), sem("pw_hi"), sem("pw_lo")
        x_in, bn_ok, mv_ok = sems("x_in"), sems("bn_ok"), sem("mv_ok")
        std_ok, rstd_ok, xn_ok = sem("std_ok"), sem("rstd_ok"), sems("xn_ok")
        t_mm, xT_hi, xT_lo = sems("t_mm"), sems("xT_hi_ok"), sems("xT_lo_ok")
        qk_mm, qk_hi, qk_lo = sems("qk_mm"), sems("qk_hi"), sems("qk_lo")
        v_mm, v_hi, v_lo = sems("v_mm"), sems("v_hi_ok"), sems("v_lo_ok")
        k_in, k_hi, k_split = sems("k_in"), sems("k_hi"), sems("k_split")
        v_in, vc_hi, v_split = sems("v_in"), sems("vc_hi"), sems("v_split")
        s_mm, max_ok, bias_ok, exp_ok = sems("s_mm"), sems("max_ok"), sems("bias_ok"), sems("exp_ok")
        inv_ok, pt_mm, pt_hi, pt_lo = sems("inv_ok"), sems("pt_mm"), sems("pt_hi"), sems("pt_lo")
        av_mm, o_ok, o_out = sems("av_mm"), sems("o_ok"), sems("o_out")
        w_in, w_used = sems("w_in"), sems("w_used")
        wabs_ok, wsum_mm, wmean_ok, wscale_ok = sem("wabs_ok"), sem("wsum_mm"), sem("wmean_ok"), sem("wscale_ok")
        wscur_ok, wround_ok = sem("wscur_ok"), sem("wround_ok")
        wo_in, wo_hi_ok, wo_lo_ok = sem("wo_in"), sem("wo_hi_ok"), sem("wo_lo_ok")
        pool_go, dve_go = sem("pool_go"), sem("dve_go")
        ot_in, xt_in = sems("ot_in"), sems("xt_in")
        ot_mm, oT_hi_ok, oT_lo_ok = sems("ot_mm"), sems("oT_hi_ok"), sems("oT_lo_ok")
        pr_mm, x1_ok, bn2_ok = sems("pr_mm"), sems("x1_ok"), sem("bn2_ok")
        mv2_ok, std2_ok, rstd2_ok, wdq_ok, wdqg_ok = sem("mv2_ok"), sem("std2_ok"), sem("rstd2_ok"), sem("wdq_ok"), sem("wdqg_ok")
        xc_ok, xamax_ok, xclip_ok, xinv_ok = sems("xc_ok"), sems("xamax_ok"), sems("xclip_ok"), sems("xinv_ok")
        xmul_ok, xdq_ok, xr_ok, xq_ok = sems("xmul_ok"), sems("xdq_ok"), sems("xr_ok"), sems("xq_ok")
        xq_mm, xqT_ok = sems("xq_mm"), sems("xqT_ok")
        ab_mm, h_ok, silu_ok = sems("ab_mm"), sems("h_ok"), sems("silu_ok")
        hamax_ok, hclip_ok, hinv_ok, hmul_ok, ydq_ok = (sems(n) for n in ("hamax_ok", "hclip_ok", "hinv_ok", "hmul_ok", "ydq_ok"))
        hr_ok, hq_ok, h_mm, hT_a, hT_b = sems("hr_ok"), sems("hq_ok"), sems("h_mm"), sems("hT_a"), sems("hT_b")
        w2_mm, y_ok, y_out = sems("w2_mm"), sems("y_ok"), sems("y_out")

        HI, LO = 0, 1
        PASSES = [(HI, HI), (HI, LO), (LO, HI)]
        Q_BANK, R_BANK, S_BANK = banks[0:2], banks[2:4], banks[4:6]
        PT_BANK, AV_BANK = banks[6], banks[7]

        XQ_PS = banks[4][:, 0:2 * P].bitcast(bf16).rearrange("p (c t) -> p c t", c=DC)
        H_PS = [banks[5][:, 0:4 * P].bitcast(bf16).rearrange("p (c t) -> p c t", c=8),
                banks[6][:, 0:3 * P // 2].bitcast(bf16).rearrange("p (c t) -> p c t", c=3)]

        def k_new(bank):
            return bank[:, 0:4 * TQ].rearrange("p (e u t) -> p u e t", e=2, u=2)

        def two(bank):
            return bank[:, 0:4 * TQ].rearrange("p (e t) -> p e t", e=2)

        def four(bank, n):
            return bank[:, 0:4 * n].rearrange("p (c t) -> p c t", c=4)

        def fr(ap):
            return ap.bitcast(fp32)

        def first_half_over(eng):
            for u in range(2):
                eng.wait_ge(o_ok[u], GROUPS)
                eng.wait_ge(o_out[u], 16 * GROUPS)

        def bank_turn(u, j):
            return (3 * u + j) % 2, (3 * u + j) // 2

        block = keep.enter_context(nc.Block())

        @block.sync
        def _(eng):
            def load_x(g, u):
                eng.wait_ge(t_mm[u], g)
                eng.dma_start(xb[:, u, :], x_b[bass.ds(2 * g + u, 1), :, :].rearrange("a t d -> (a t) d")).then_inc(x_in[u], 16)

            def load_k(g, u):
                if not (isinstance(g, int) and g == 0 and u == 0):
                    eng.wait_ge(k_split[1 - u], g + u)
                eng.dma_start(kraw[:, :, :], ctxT[bass.ds(2 * g + u, 1), :, :, :].rearrange("a p c k -> (a p) c k")).then_inc(k_in[u], 16)

            def load_v(g, u):
                if not (isinstance(g, int) and g == 0 and u == 0):
                    eng.wait_ge(v_split[1 - u], g + u)
                eng.dma_start(vraw[:, :, :], ctx[bass.ds(2 * g + u, 1), :, :, :].rearrange("a p c d -> (a p) c d")).then_inc(v_in[u], 16)

            def load_w(chunk, turn, j):
                eng.wait_ge(w_used[j % 2], turn + j // 2)
                eng.dma_start(wbuf[:, j % 2, :], wffn[bass.ds(chunk + j, 1), :, :].rearrange("a p f -> (a p) f")).then_inc(w_in[j % 2], 16)

            def store_o(g, u):
                eng.wait_ge(o_ok[u], g + 1)
                eng.dma_start(o_b[bass.ds(2 * g + u, 1), :, :].rearrange("a t d -> (a t) d"), ob[:, u, :]).then_inc(o_out[u], 16)

            def group(g, w=None):
                if w:
                    load_w(*w, 0)
                load_x(g + 1, 0)
                load_x(g + 1, 1)
                load_k(g + 1, 0)
                if w:
                    load_w(*w, 1)
                load_v(g + 1, 0)
                load_k(g + 1, 1)
                if w:
                    load_w(*w, 2)
                load_v(g + 1, 1)
                if w:
                    load_w(*w, 3)
                store_o(g, 0)
                store_o(g, 1)

            for u in range(2):
                eng.dma_start(xb[:, u, :], x_b[u, :, :]).then_inc(x_in[u], 16)
            eng.dma_start(gin[0:1, 0:1], g_xattn.rearrange("(a b) -> a b", a=1)).then_inc(g_in, 16)
            eng.dma_start(gin[0:1, 1:2], g_ffn.rearrange("(a b) -> a b", a=1)).then_inc(g_in, 16)
            eng.dma_start(wraw[:, 0, :, :], wqT).then_inc(pw_in[0], 16)
            eng.dma_start(wraw[:, 1, :, :], wkT).then_inc(pw_in[1], 16)
            load_k(0, 0)
            eng.dma_start(wraw[:, 2, :, :], wvT).then_inc(pw_in[2], 16)
            load_v(0, 0)
            load_k(0, 1)
            load_v(0, 1)
            group(0, (0, 0))
            with eng.Fori(1, 3) as g:
                group(g, (4 * g, 2 * g))
            group(3)
            with eng.Fori(4, 7) as g:
                group(g, (4 * g - 16, 2 * g - 2))
            for s in w_used:
                eng.wait_ge(s, 12)
            eng.dma_start(wbuf[:, :, :].rearrange("p a f -> p (a f)")[:, 0:DC * D].rearrange("p (c n) -> p c n", c=DC), woT).then_inc(wo_in, 16)
            store_o(7, 0)
            store_o(7, 1)

            first_half_over(eng)
            def load_tile(i, u):
                eng.wait_ge(ot_mm[u], i)
                eng.dma_start(ot[:, u, :], o_t[bass.ds(2 * i + u, 1), :, :].rearrange("a p d -> (a p) d")).then_inc(ot_in[u], 16)
                eng.wait_ge(x1_ok[u], i)
                eng.dma_start(xt[:, u, :], x_t[bass.ds(2 * i + u, 1), :, :].rearrange("a p d -> (a p) d")).then_inc(xt_in[u], 16)

            load_tile(0, 0)
            load_tile(0, 1)
            with eng.Fori(1, PAIRS) as i:
                load_tile(i, 0)
                load_tile(i, 1)
            with eng.Fori(0, PAIRS) as i:
                for u in range(2):
                    eng.wait_ge(y_ok[u], i + 1)
                    eng.dma_start(y_t[bass.ds(2 * i + u, 1), :, :].rearrange("a p d -> (a p) d"), yb[:, u, :]).then_inc(y_out[u], 16)
            for u in range(2):
                eng.wait_ge(y_out[u], 16 * PAIRS)

        @block.gpsimd
        def _(eng):
            eng.memset(ident[:, :], 0.0).then_inc(consts, 1)
            eng.memset(identb[:, :], 0.0).then_inc(consts, 1)
            eng.memset(ones[:, :], 1.0).then_inc(consts, 1)
            eng.memset(magic[:, 0:1], MAGIC).then_inc(consts, 1)
            eng.memset(magic[:, 1:2], -MAGIC).then_inc(consts, 1)
            eng.memset(epsc[:, :], EPS).then_inc(consts, 1)
            for half in kT:
                eng.memset(half[:, :, :, KEYS:KPAD].bitcast(fp32), 0.0).then_inc(consts, 1)
            eng.memset(prob[:, :, KEYS:PPAD], 0.0).then_inc(consts, 1)
            eng.wait_ge(consts, 9)
            for m in (ident, identb):
                eng.affine_select(out=m[:, :], in_=m[:, :], compare_op=ALU.not_equal, fill=1.0,
                                  base=0, pattern=[[-1, P]], channel_multiplier=1).then_inc(consts, 1)
            def split(g, u):
                eng.wait_ge(k_in[u], 16 * g + 16)
                eng.wait_ge(s_mm[u], g)
                eng.sem_inc(pool_go, 1)
                eng.tensor_scalar(kT[HI][:, u, :, 0:KC], kraw[:, :, :], 1.0, 0.0, ALU.mult, ALU.add).then_inc(k_hi[u], 1)
                eng.wait_ge(k_hi[u], g + 1)
                eng.tensor_tensor(kT[LO][:, u, :, 0:KC], kraw[:, :, :], fr(kT[HI][:, u, :, 0:KC]), ALU.subtract).then_inc(k_split[u], 1)
                eng.wait_ge(pw_lo, 3)
                eng.wait_ge(v_in[u], 16 * g + 16)
                eng.wait_ge(av_mm[u], g)
                eng.sem_inc(pool_go, 1)
                eng.tensor_scalar(vv[HI][0:CK, u, 0:3, :], vraw[:, :, :], 1.0, 0.0, ALU.mult, ALU.add).then_inc(vc_hi[u], 1)
                eng.wait_ge(vc_hi[u], g + 1)
                eng.tensor_tensor(vv[LO][0:CK, u, 0:3, :], vraw[:, :, :], fr(vv[HI][0:CK, u, 0:3, :]), ALU.subtract).then_inc(v_split[u], 1)

            for u in range(2):
                split(0, u)
            with eng.Fori(1, GROUPS) as g:
                for u in range(2):
                    split(g, u)

            def quant_x(i, u):
                eng.wait_ge(xmul_ok[u], i + 1)
                eng.sem_inc(pool_go, 1)
                eng.tensor_scalar(xc[:, u, :], xc[:, u, :], col["xmul"][:, u:u + 1], MAGIC, ALU.mult, ALU.add).then_inc(xr_ok[u], 1)
                eng.wait_ge(xr_ok[u], i + 1)
                eng.wait_ge(xq_mm[u], i)
                eng.sem_inc(pool_go, 1)
                eng.tensor_scalar(xq[:, u, :], xc[:, u, :], -MAGIC, 1.0, ALU.add, ALU.mult).then_inc(xq_ok[u], 1)

            def quant_h(i, u):
                eng.wait_ge(hr_ok[u], i + 1)
                eng.wait_ge(h_mm[u], i)
                eng.sem_inc(pool_go, 1)
                eng.tensor_scalar(hq[:, u, :], hid[:, u, :], -MAGIC, 1.0, ALU.add, ALU.mult).then_inc(hq_ok[u], 1)

            for u in range(2):
                quant_x(0, u)
            for u in range(2):
                quant_h(0, u)
                quant_x(1, u)
            with eng.Fori(1, PAIRS - 1) as i:
                for u in range(2):
                    quant_h(i, u)
                    quant_x(i + 1, u)
            for u in range(2):
                quant_h(PAIRS - 1, u)

        @block.scalar
        def _(act):
            def std_of(g):
                act.wait_ge(mv_ok, 2 * g + 2)
                nc.scalar.activation(std[:, :], mv[:, :, 1], ACT.Sqrt, bias=epsc[0:TQ, 0:1]).then_inc(std_ok, 1)

            def x_hi(g, u):
                act.wait_ge(t_mm[u], g + 1)
                act.wait_ge(v_mm[0], g)
                act.wait_ge(v_mm[1], g)
                nc.scalar.copy(xT[HI][:, :, u * TQ:(u + 1) * TQ], four(R_BANK[u], TQ)).then_inc(xT_hi[u], 1)

            def qk(g, j):
                act.wait_ge(qk_mm[j % 2], 2 * g + j // 2 + 1)
                if j == 0:
                    for u in range(2):
                        act.wait_ge(s_mm[u], g)
                if j < 2:
                    nc.scalar.copy(qT[HI][:, 2 * j:2 * j + 2, :], two(Q_BANK[j % 2])).then_inc(qk_hi[j % 2], 1)
                else:
                    e = 2 * (j - 2)
                    nc.scalar.copy(kT[HI][:, :, e:e + 2, KC:KEYS], k_new(Q_BANK[j % 2])).then_inc(qk_hi[j % 2], 1)

            def v(g, u):
                act.wait_ge(v_mm[u], g + 1)
                act.wait_ge(av_mm[u], g)
                act.wait_ge(pw_lo, 3)
                nc.scalar.copy(vv[HI][0:TQ, u, 3, :], R_BANK[u][0:TQ, :]).then_inc(v_hi[u], 1)

            def exp(g, u):
                act.wait_ge(bias_ok[u], g + 1)
                act.wait_ge(pt_mm[u], g)
                nc.scalar.activation(prob[:, u, 0:KEYS], S_BANK[u][0:TQ, 0:KEYS], ACT.Exp, bias=expbias[:, u:u + 1],
                                     scale=SCALE, accum_out=rowsum[:, u:u + 1]).then_inc(exp_ok[u], 1)

            def pt(g, u):
                act.wait_ge(pt_mm[u], g + 1)
                act.wait_ge(av_mm[u], g)
                nc.scalar.copy(pT[HI][:, u, :], PT_BANK[0:CK, 0:4 * TQ]).then_inc(pt_hi[u], 1)

            def o(g, u):
                act.wait_ge(av_mm[u], g + 1)
                act.wait_ge(inv_ok[u], g + 1)
                act.wait_ge(o_out[u], 16 * g)
                nc.scalar.activation(ob[:, u, :], AV_BANK[0:TQ, :], ACT.Copy, scale=rowinv[:, u:u + 1]).then_inc(o_ok[u], 1)

            def ternary(g, turn, j):
                s = j % 2
                act.wait_ge(w_in[s], 16 * (turn + j // 2) + 16)
                nc.scalar.activation(wbuf[:, s, :], wbuf[:, s, :], ACT.Identity, bias=magic[:, 0:1],
                                     scale=wscur[:, 0:1]).then_inc(wround_ok, 1)
                act.wait_ge(wround_ok, 4 * g - 16 + j + 1)
                nc.scalar.activation(WQ[:, bass.ds(4 * g - 16 + j, 1), :].rearrange("p a f -> p (a f)"), wbuf[:, s, :],
                                     ACT.Sign, bias=magic[:, 1:2]).then_inc(w_used[s], 1)

            def group(g, w=False, last=False):
                if w:
                    act.wait_ge(wscale_ok, 1)
                    act.wait_ge(w_used[1], 2 * g - 2)
                    nc.scalar.copy(wscur[:, 0:1], wscale[:, bass.ds(g - 4, 1)]).then_inc(wscur_ok, 1)
                    act.wait_ge(wscur_ok, g - 3)
                qk(g, 0)
                if w:
                    ternary(g, 2 * g - 2, 0)
                qk(g, 1)
                if not last:
                    std_of(g + 1)
                qk(g, 2)
                if w:
                    ternary(g, 2 * g - 2, 1)
                qk(g, 3)
                v(g, 0)
                exp(g, 0)
                if w:
                    ternary(g, 2 * g - 2, 2)
                v(g, 1)
                pt(g, 0)
                exp(g, 1)
                if w:
                    ternary(g, 2 * g - 2, 3)
                o(g, 0)
                pt(g, 1)
                if last:
                    act.wait_ge(wo_in, 16)
                    for s in qk_mm:
                        act.wait_ge(s, 2 * GROUPS)
                    nc.scalar.copy(wo[HI][:, :, :], raw_wo).then_inc(wo_hi_ok, 1)
                else:
                    x_hi(g + 1, 0)
                    x_hi(g + 1, 1)
                o(g, 1)

            raw_wo = wbuf[:, :, :].rearrange("p a f -> p (a f)")[:, 0:DC * D].rearrange("p (c n) -> p c n", c=DC)
            act.wait_ge(tanh_mm, 1)
            nc.scalar.activation(gates[:, :], AV_BANK[:, 0:2], ACT.Tanh).then_inc(gates_ok, 1)
            act.wait_ge(consts, 11)
            std_of(0)
            for i in range(3):
                act.wait_ge(pw_in[i], 16)
                nc.scalar.copy(wsp[i][HI][:, :, :], wraw[:, i, :, :]).then_inc(pw_hi, 1)
                if i == 0:
                    x_hi(0, 0)
                    x_hi(0, 1)
            group(0)
            with act.Fori(1, 3) as g:
                group(g)
            group(3)
            with act.Fori(4, 7) as g:
                group(g, w=True)
            group(7, last=True)

            first_half_over(act)

            def oT_high(i, u):
                act.wait_ge(ot_mm[u], i + 1)
                act.wait_ge(pr_mm[u], i)
                nc.scalar.copy(oT[HI][:, u, :, :], four(banks[u], P)).then_inc(oT_hi_ok[u], 1)

            oT_high(0, 0)
            oT_high(0, 1)
            with act.Fori(1, PAIRS) as i:
                oT_high(i, 0)
                oT_high(i, 1)
            act.wait_ge(mv2_ok, NT)
            nc.scalar.activation(std2[:, :], mv2[:, :, 1], ACT.Sqrt, bias=epsc[:, 0:1]).then_inc(std2_ok, 1)

            def center(i, u):
                act.wait_ge(xq_ok[u], i)
                nc.scalar.activation(xc[:, u, :], x1[:, bass.ds(2 * i + u, 1), :].rearrange("p a d -> p (a d)"),
                                     ACT.Identity, bias=nmean2[:, bass.ds(2 * i + u, 1)]).then_inc(xc_ok[u], 1)

            def silu(i, u, j):
                c, n = HCH[j]
                k, turn = bank_turn(u, j)
                act.wait_ge(ab_mm[k], 3 * i + turn + 1)
                if j == 0:
                    act.wait_ge(xdq_ok[u], i + 1)
                    act.wait_ge(hq_ok[u], i)
                nc.scalar.activation(hid[:, u, c:c + n], banks[k][:, 0:n], ACT.Silu,
                                     scale=xdq[:, u, 0:1]).then_inc(silu_ok[u], 1)

            def xqT_copy(i, u):
                act.wait_ge(xq_mm[u], i + 1)
                nc.scalar.copy(xqT[:, u, :, :], XQ_PS).then_inc(xqT_ok[u], 1)

            def hT_copy(i, u):
                act.wait_ge(h_mm[u], i + 1)
                act.wait_ge(w2_mm[u], i)
                nc.scalar.copy(hqT[:, u, 0:8, :], H_PS[0]).then_inc(hT_a[u], 1)

            def round_h(i, u):
                act.wait_ge(hmul_ok[u], i + 1)
                nc.scalar.activation(hid[:, u, :], hid[:, u, :], ACT.Identity, bias=magic[:, 0:1],
                                     scale=col["hmul"][:, u:u + 1]).then_inc(hr_ok[u], 1)

            def tile(i, u, first=False, last=False, more=True):
                for j in range(3):
                    silu(i, u, j)
                if more:
                    center(i + 1, u)
                if not last:
                    xqT_copy(i + u, 1 - u)
                if not first:
                    hT_copy(i + u - 1, 1 - u)
                round_h(i, u)

            act.wait_ge(rstd2_ok, 1)
            center(0, 0)
            center(0, 1)
            xqT_copy(0, 0)
            tile(0, 0, first=True)
            tile(0, 1)
            with act.Fori(1, PAIRS - 1) as i:
                tile(i, 0)
                tile(i, 1)
            tile(PAIRS - 1, 0, more=False)
            tile(PAIRS - 1, 1, last=True, more=False)
            hT_copy(PAIRS - 1, 1)

        @block.vector
        def _(dve):
            V = nc.vector

            def stats(g):
                for u in range(2):
                    dve.wait_ge(x_in[u], 16 * g + 16)
                    V.bn_stats(bn[:, u, :], xb[:, u, :]).then_inc(bn_ok[u], 1)
                    dve.wait_ge(bn_ok[u], g + 1)
                    dve.sem_inc(dve_go, 1)
                    V.bn_aggr(mv[:, u, :], bn[:, u, :]).then_inc(mv_ok, 1)

            def normalise(g):
                dve.wait_ge(std_ok, g + 1)
                V.reciprocal(rstd[:, :], std[:, :]).then_inc(rstd_ok, 1)
                dve.wait_ge(rstd_ok, g + 1)
                for u in range(2):
                    V.tensor_scalar(xb[:, u, :], xb[:, u, :], mv[:, u, 0:1], rstd[:, u:u + 1],
                                    ALU.subtract, ALU.mult).then_inc(xn_ok[u], 1)

            def x_lo(g, u):
                dve.wait_ge(xT_hi[u], g + 1)
                d = slice(u * TQ, (u + 1) * TQ)
                V.tensor_tensor(xT[LO][:, :, d], four(R_BANK[u], TQ), fr(xT[HI][:, :, d]), ALU.subtract).then_inc(xT_lo[u], 1)

            def qk(g, j):
                dve.wait_ge(qk_hi[j % 2], 2 * g + j // 2 + 1)
                if j < 2:
                    d = slice(2 * j, 2 * j + 2)
                    V.tensor_tensor(qT[LO][:, d, :], two(Q_BANK[j % 2]), fr(qT[HI][:, d, :]), ALU.subtract).then_inc(qk_lo[j % 2], 1)
                else:
                    e = 2 * (j - 2)
                    V.tensor_tensor(kT[LO][:, :, e:e + 2, KC:KEYS], k_new(Q_BANK[j % 2]),
                                    fr(kT[HI][:, :, e:e + 2, KC:KEYS]), ALU.subtract).then_inc(qk_lo[j % 2], 1)

            def v(g, u):
                dve.wait_ge(v_hi[u], g + 1)
                V.tensor_tensor(vv[LO][0:TQ, u, 3, :], R_BANK[u][0:TQ, :], fr(vv[HI][0:TQ, u, 3, :]),
                                ALU.subtract).then_inc(v_lo[u], 1)

            def rowmaxima(g, u):
                dve.wait_ge(s_mm[u], g + 1)
                V.tensor_reduce(rowmax[:, u:u + 1], S_BANK[u][0:TQ, 0:KEYS], AX, ALU.max).then_inc(max_ok[u], 1)
                dve.wait_ge(max_ok[u], g + 1)
                dve.wait_ge(exp_ok[u], g)
                V.tensor_scalar(expbias[:, u:u + 1], rowmax[:, u:u + 1], -SCALE, None, ALU.mult).then_inc(bias_ok[u], 1)

            def pt(g, u):
                dve.wait_ge(pt_hi[u], g + 1)
                V.tensor_tensor(pT[LO][:, u, :], PT_BANK[0:CK, 0:4 * TQ], fr(pT[HI][:, u, :]), ALU.subtract).then_inc(pt_lo[u], 1)
                dve.wait_ge(exp_ok[u], g + 1)
                dve.wait_ge(o_ok[u], g)
                V.reciprocal(rowinv[:, u:u + 1], rowsum[:, u:u + 1]).then_inc(inv_ok[u], 1)

            def magnitudes(g, j):
                dve.wait_ge(w_in[j % 2], 16 * (2 * g + j // 2) + 16)
                V.tensor_reduce(wabs[:, bass.ds(4 * g + j, 1)], wbuf[:, j % 2, :], AX, ALU.add,
                                apply_absolute_value=True).then_inc(w_used[j % 2], 1)

            def group(g, w=False, scales=False, last=False):
                qk(g, 0)
                if not last:
                    stats(g + 1)
                qk(g, 1)
                if w:
                    magnitudes(g, 0)
                qk(g, 2)
                if not last:
                    normalise(g + 1)
                if w:
                    magnitudes(g, 1)
                qk(g, 3)
                if scales:
                    for s in w_used:
                        dve.wait_ge(s, 6)
                    V.tensor_reduce(wabs3[:, :], wabs[:, :].rearrange("p (m c) -> p m c", c=4), AX, ALU.add).then_inc(wabs_ok, 1)
                v(g, 0)
                rowmaxima(g, 0)
                v(g, 1)
                if w:
                    magnitudes(g, 2)
                pt(g, 0)
                rowmaxima(g, 1)
                if w:
                    magnitudes(g, 3)
                pt(g, 1)
                if scales:
                    dve.wait_ge(wsum_mm, 1)
                    V.tensor_scalar(wmean[:, :], AV_BANK[:, 0:3], 1.0 / NW, EPS, ALU.mult, ALU.max).then_inc(wmean_ok, 1)
                    dve.wait_ge(wmean_ok, 1)
                    V.reciprocal(wscale[:, :], wmean[:, :]).then_inc(wscale_ok, 1)
                if last:
                    dve.wait_ge(wo_hi_ok, 1)
                    V.tensor_tensor(wo[LO][:, :, :], raw_wo, fr(wo[HI][:, :, :]), ALU.subtract).then_inc(wo_lo_ok, 1)
                else:
                    x_lo(g + 1, 0)
                    x_lo(g + 1, 1)

            raw_wo = wbuf[:, :, :].rearrange("p a f -> p (a f)")[:, 0:DC * D].rearrange("p (c n) -> p c n", c=DC)
            stats(0)
            normalise(0)
            for i in range(3):
                dve.wait_ge(pw_hi, i + 1)
                V.tensor_tensor(wsp[i][LO][:, :, :], wraw[:, i, :, :], fr(wsp[i][HI][:, :, :]), ALU.subtract).then_inc(pw_lo, 1)
                if i == 0:
                    x_lo(0, 0)
                    x_lo(0, 1)
            group(0, w=True)
            with dve.Fori(1, 3) as g:
                group(g, w=True)
            group(3, scales=True)
            with dve.Fori(4, 7) as g:
                group(g)
            group(7, last=True)

            first_half_over(dve)
            V.tensor_scalar(wdq[:, 0:2], wmean[:, 0:2], 1.0 / 127.0, None, ALU.mult).then_inc(wdq_ok, 1)
            dve.wait_ge(gates_ok, 1)
            V.tensor_scalar(wdq[:, 2:3], wmean[:, 2:3], 1.0 / 127.0, gates[:, 1:2], ALU.mult, ALU.mult).then_inc(wdq_ok, 1)

            def oT_low(i, u):
                dve.wait_ge(oT_hi_ok[u], i + 1)
                V.tensor_tensor(oT[LO][:, u, :, :], four(banks[u], P), fr(oT[HI][:, u, :, :]), ALU.subtract).then_inc(oT_lo_ok[u], 1)

            def add(i, u):
                dve.wait_ge(pr_mm[u], i + 1)
                dve.wait_ge(xt_in[u], 16 * i + 16)
                t = x1[:, bass.ds(2 * i + u, 1), :].rearrange("p a d -> p (a d)")
                V.scalar_tensor_tensor(out=t, in0=banks[2 + u][:, :], scalar=gates[:, 0:1], in1=xt[:, u, :],
                                       op0=ALU.mult, op1=ALU.add).then_inc(x1_ok[u], 1)
                dve.wait_ge(x1_ok[u], i + 1)
                V.bn_stats(bn2[:, bass.ds(12 * i + 6 * u, 6)], t).then_inc(bn2_ok, 1)

            def pair(i):
                oT_low(i, 1)
                add(i, 0)
                oT_low(i + 1, 0)
                add(i, 1)

            oT_low(0, 0)
            pair(0)
            with dve.Fori(1, PAIRS - 1) as i:
                pair(i)
            oT_low(PAIRS - 1, 1)
            add(PAIRS - 1, 0)
            add(PAIRS - 1, 1)
            dve.wait_ge(bn2_ok, NT)
            for t in range(NT):
                V.bn_aggr(mv2[:, t, :], bn2[:, 6 * t:6 * t + 6]).then_inc(mv2_ok, 1)
            dve.wait_ge(mv2_ok, NT)
            V.tensor_scalar(nmean2[:, :], mv2[:, :, 0], -1.0, None, ALU.mult).then_inc(rstd2_ok, 1)
            dve.wait_ge(std2_ok, 1)
            V.reciprocal(rstd2[:, :], std2[:, :]).then_inc(rstd2_ok, 1)
            dve.wait_ge(rstd2_ok, 2)
            dve.wait_ge(wdq_ok, 2)

            c = {n: (lambda a: (lambda u: a[:, u:u + 1]))(a) for n, a in col.items()}

            def x_scale(i, u):
                r = rstd2[:, bass.ds(2 * i + u, 1)]
                dve.wait_ge(xc_ok[u], i + 1)
                V.tensor_reduce(c["xamax"](u), xc[:, u, :], AX, ALU.max, apply_absolute_value=True).then_inc(xamax_ok[u], 1)
                dve.wait_ge(xamax_ok[u], i + 1)
                V.tensor_scalar(c["xclip"](u), c["xamax"](u), r, EPS, ALU.mult, ALU.max).then_inc(xclip_ok[u], 1)
                dve.wait_ge(xclip_ok[u], i + 1)
                V.reciprocal(c["xinv"](u), c["xclip"](u)).then_inc(xinv_ok[u], 1)
                V.tensor_scalar(xdq[:, u, :], wdq[:, 0:2], c["xclip"](u), None, ALU.mult).then_inc(xdq_ok[u], 1)
                dve.wait_ge(xinv_ok[u], i + 1)
                V.tensor_scalar(c["xmul"](u), c["xinv"](u), 127.0, r, ALU.mult, ALU.mult).then_inc(xmul_ok[u], 1)

            def hidden(i, u):
                for j, (a, n) in enumerate(HCH):
                    k, turn = bank_turn(u, j)
                    dve.wait_ge(silu_ok[u], 3 * i + j + 1)
                    dve.wait_ge(xdq_ok[u], i + 1)
                    V.scalar_tensor_tensor(out=hid[:, u, a:a + n], in0=banks[2 + k][:, 0:n], scalar=xdq[:, u, 1:2],
                                           in1=hid[:, u, a:a + n], op0=ALU.mult, op1=ALU.mult).then_inc(h_ok[k], 1)

            def h_scale(i, u):
                dve.wait_ge(h_ok[0], 3 * i + (2 if u == 0 else 3))
                dve.wait_ge(h_ok[1], 3 * i + (1 if u == 0 else 3))
                V.tensor_reduce(c["hamax"](u), hid[:, u, :], AX, ALU.max, apply_absolute_value=True).then_inc(hamax_ok[u], 1)
                dve.wait_ge(hamax_ok[u], i + 1)
                V.tensor_scalar(c["hclip"](u), c["hamax"](u), EPS, None, ALU.max).then_inc(hclip_ok[u], 1)
                dve.wait_ge(hclip_ok[u], i + 1)
                V.reciprocal(c["hinv"](u), c["hclip"](u)).then_inc(hinv_ok[u], 1)
                V.tensor_scalar(c["ydq"](u), c["hclip"](u), wdq[:, 2:3], None, ALU.mult).then_inc(ydq_ok[u], 1)
                dve.wait_ge(hinv_ok[u], i + 1)
                V.tensor_scalar(c["hmul"](u), c["hinv"](u), 127.0, None, ALU.mult).then_inc(hmul_ok[u], 1)

            def hT_copy(i, u):
                dve.wait_ge(h_mm[u], i + 1)
                dve.wait_ge(w2_mm[u], i)
                V.tensor_copy(hqT[:, u, 8:FC, :], H_PS[1]).then_inc(hT_b[u], 1)

            def result(i, u):
                dve.wait_ge(w2_mm[u], i + 1)
                dve.wait_ge(ydq_ok[u], i + 1)
                dve.wait_ge(y_out[u], 16 * i)
                V.scalar_tensor_tensor(out=yb[:, u, :], in0=banks[7][:, :], scalar=c["ydq"](u),
                                       in1=x1[:, bass.ds(2 * i + u, 1), :].rearrange("p a d -> p (a d)"),
                                       op0=ALU.mult, op1=ALU.add).then_inc(y_ok[u], 1)

            def tile(i, u, first=False, more=True):
                hidden(i, u)
                if not first:
                    hT_copy(i + u - 1, 1 - u)
                h_scale(i, u)
                if more:
                    x_scale(i + 1, u)
                if not first:
                    result(i + u - 1, 1 - u)

            x_scale(0, 0)
            x_scale(0, 1)
            tile(0, 0, first=True)
            tile(0, 1)
            with dve.Fori(1, PAIRS - 1) as i:
                tile(i, 0)
                tile(i, 1)
            tile(PAIRS - 1, 0, more=False)
            tile(PAIRS - 1, 1, more=False)
            hT_copy(PAIRS - 1, 1)
            result(PAIRS - 1, 1)

        @block.tensor
        def _(pe):
            def products(dst, pairs):
                for n, (a, b) in enumerate(pairs):
                    ins = nc.tensor.matmul(dst, a, b, start=(n == 0), stop=(n == len(pairs) - 1))
                return ins

            def transpose_x(g, u):
                pe.wait_ge(xn_ok[u], g + 1)
                pe.wait_ge(v_lo[u], g)
                for c in range(DC):
                    ins = nc.tensor.transpose(R_BANK[u][:, c * TQ:(c + 1) * TQ], xb[:, u, c * P:(c + 1) * P], ident[0:TQ, 0:TQ])
                ins.then_inc(t_mm[u], 1)

            def qk(g):
                for u in range(2):
                    pe.wait_ge(xT_lo[u], g + 1)
                for j in range(4):
                    if j % 2 == 0:
                        pe.wait_ge(pw_lo, 1 + j // 2)
                    pe.wait_ge(qk_lo[j % 2], 2 * g + j // 2)
                    w = wsp[j // 2]
                    for e in range(2):
                        o = 2 * (j % 2) + e
                        ins = products(Q_BANK[j % 2][:, e * 2 * TQ:(e + 1) * 2 * TQ],
                                       [(w[a][:, c, o * P:(o + 1) * P], xT[b][:, c, :]) for c in range(DC) for a, b in PASSES])
                    ins.then_inc(qk_mm[j % 2], 1)

            def v(g, u):
                pe.wait_ge(pw_lo, 3)
                products(R_BANK[u][0:TQ, :], [(xT[a][:, c, u * TQ:(u + 1) * TQ], wsp[2][b][:, c, :])
                                              for c in range(DC) for a, b in PASSES]).then_inc(v_mm[u], 1)

            def scores(g, u):
                for s in qk_lo:
                    pe.wait_ge(s, 2 * g + 2)
                pe.wait_ge(k_split[u], g + 1)
                pe.wait_ge(exp_ok[u], g)
                products(S_BANK[u][0:TQ, 0:KPAD], [(qT[a][:, c, u * TQ:(u + 1) * TQ], kT[b][:, u, c, :])
                                                   for c in range(DC) for a, b in PASSES]).then_inc(s_mm[u], 1)

            def transpose_p(g, u):
                pe.wait_ge(exp_ok[u], g + 1)
                pe.wait_ge(pt_lo[1 - u], g + u)
                for c in range(4):
                    ins = nc.tensor.transpose(PT_BANK[0:CK, c * TQ:(c + 1) * TQ], prob[:, u, c * CK:(c + 1) * CK], ident[0:TQ, 0:TQ])
                ins.then_inc(pt_mm[u], 1)

            def values(g, u):
                pe.wait_ge(pt_lo[u], g + 1)
                pe.wait_ge(v_lo[u], g + 1)
                pe.wait_ge(v_split[u], g + 1)
                pe.wait_ge(o_ok[1 - u], g + u)
                n = [CK, CK, CK, TQ]
                products(AV_BANK[0:TQ, :], [(pT[a][0:n[c], u, c * TQ:(c + 1) * TQ], vv[b][0:n[c], u, c, :])
                                            for c in range(4) for a, b in PASSES]).then_inc(av_mm[u], 1)

            def group(g, scales=False, last=False):
                qk(g)
                v(g, 0)
                scores(g, 0)
                v(g, 1)
                transpose_p(g, 0)
                scores(g, 1)
                values(g, 0)
                transpose_p(g, 1)
                if not last:
                    transpose_x(g + 1, 0)
                    transpose_x(g + 1, 1)
                if scales:
                    pe.wait_ge(wabs_ok, 1)
                    pe.wait_ge(o_ok[0], g + 1)
                    nc.tensor.matmul(AV_BANK[:, 0:3], ones[:, :], wabs3[:, :], start=True, stop=True).then_inc(wsum_mm, 1)
                    pe.wait_ge(wmean_ok, 1)
                values(g, 1)

            pe.wait_ge(consts, 11)
            pe.wait_ge(g_in, 32)
            nc.tensor.matmul(AV_BANK[:, 0:2], ones[0:1, :], gin[0:1, :], start=True, stop=True).then_inc(tanh_mm, 1)
            transpose_x(0, 0)
            transpose_x(0, 1)
            pe.wait_ge(gates_ok, 1)
            group(0)
            with pe.Fori(1, 3) as g:
                group(g)
            group(3, scales=True)
            with pe.Fori(4, 7) as g:
                group(g)
            group(7, last=True)

            def transpose_o(i, u):
                pe.wait_ge(ot_in[u], 16 * i + 16)
                pe.wait_ge(oT_lo_ok[u], i)
                for c in range(DC):
                    ins = nc.tensor.transpose(banks[u][:, c * P:(c + 1) * P], ot[:, u, c * P:(c + 1) * P], ident[:, :])
                ins.then_inc(ot_mm[u], 1)

            def project(i, u):
                pe.wait_ge(oT_lo_ok[u], i + 1)
                pe.wait_ge(wo_lo_ok, 1)
                pe.wait_ge(x1_ok[u], i)
                products(banks[2 + u][:, :], [(oT[a][:, u, c, :], wo[b][:, c, :])
                                              for c in range(DC) for a, b in PASSES]).then_inc(pr_mm[u], 1)

            first_half_over(pe)
            def pair(i):
                transpose_o(i, 1)
                project(i, 0)
                transpose_o(i + 1, 0)
                project(i, 1)

            transpose_o(0, 0)
            pair(0)
            with pe.Fori(1, PAIRS - 1) as i:
                pair(i)
            transpose_o(PAIRS - 1, 1)
            project(PAIRS - 1, 0)
            project(PAIRS - 1, 1)

            def transpose_xq(i, u):
                pe.wait_ge(xq_ok[u], i + 1)
                pe.wait_ge(xqT_ok[1 - u], i + u)
                for c in range(DC):
                    ins = nc.tensor.transpose(XQ_PS[:, c, :], xq[:, u, c * P:(c + 1) * P], identb[:, :])
                ins.then_inc(xq_mm[u], 1)

            def up(i, u):
                pe.wait_ge(xqT_ok[u], i + 1)
                for j, (a, n) in enumerate(HCH):
                    k, turn = bank_turn(u, j)
                    pe.wait_ge(h_ok[k], 3 * i + turn)
                    products(banks[k][:, 0:n], [(xqT[:, u, c, :], WQ[:, c, a:a + n]) for c in range(DC)])
                    products(banks[2 + k][:, 0:n], [(xqT[:, u, c, :], WQ[:, 4 + c, a:a + n])
                                                    for c in range(DC)]).then_inc(ab_mm[k], 1)

            def down(i, u):
                pe.wait_ge(hq_ok[u], i + 1)
                pe.wait_ge(hT_a[1 - u], i + u)
                pe.wait_ge(hT_b[1 - u], i + u)
                for c in range(FC):
                    ins = nc.tensor.transpose(H_PS[c // 8][:, c % 8, :], hq[:, u, c * P:(c + 1) * P], identb[:, :])
                ins.then_inc(h_mm[u], 1)
                pe.wait_ge(hT_a[u], i + 1)
                pe.wait_ge(hT_b[u], i + 1)
                pe.wait_ge(y_ok[1 - u], i + u)
                products(banks[7][:, :], [(hqT[:, u, c, :], w2q[:, c, :]) for c in range(FC)]).then_inc(w2_mm[u], 1)

            def tile(i, u, first=False, last=False):
                up(i, u)
                if not last:
                    transpose_xq(i + u, 1 - u)
                if not first:
                    down(i + u - 1, 1 - u)

            for s in x1_ok:
                pe.wait_ge(s, PAIRS)
            pe.wait_ge(gates_ok, 1)
            transpose_xq(0, 0)
            tile(0, 0, first=True)
            tile(0, 1)
            with pe.Fori(1, PAIRS - 1) as i:
                tile(i, 0)
                tile(i, 1)
            tile(PAIRS - 1, 0)
            tile(PAIRS - 1, 1, last=True)
            down(PAIRS - 1, 1)


def kernel(x, ctx_2048, mask_BxSx4224_bf0, g_xattn, g_ffn, L0_xattn_wq, L0_xattn_wk, L0_xattn_wv, L0_xattn_wo,
           L0_ffn_w1, L0_ffn_w2, L0_ffn_w3):
    import concourse.bacc as bacc
    from concourse.bass_utils import run_bass_kernel_spmd

    def chunks(w):
        w = np.asarray(w)
        return np.ascontiguousarray(w.T.reshape(w.shape[1] // P, P, w.shape[0]).transpose(1, 0, 2))

    c = np.asarray(ctx_2048)
    keys = c.reshape(B, CK, 3, DC, P).transpose(0, 4, 3, 2, 1).reshape(B, P, DC, KC)
    ffn = np.concatenate([chunks(L0_ffn_w1).transpose(1, 0, 2), chunks(L0_ffn_w3).transpose(1, 0, 2),
                          chunks(L0_ffn_w2).reshape(P, 4, F).transpose(1, 0, 2)])
    arrays = {
        "x": np.ascontiguousarray(np.asarray(x).reshape(TOK, D)),
        "ctxT": np.ascontiguousarray(keys),
        "ctx": np.ascontiguousarray(c.reshape(B, CK, 3, D)),
        "g_xattn": np.ascontiguousarray(g_xattn),
        "g_ffn": np.ascontiguousarray(g_ffn),
        "wqT": chunks(L0_xattn_wq), "wkT": chunks(L0_xattn_wk), "wvT": chunks(L0_xattn_wv), "woT": chunks(L0_xattn_wo),
        "wffn": np.ascontiguousarray(ffn),
    }
    nc = bacc.Bacc("TRN2", target_bir_lowering=False, num_devices=1)
    ins = [nc.dram_tensor(n, a.shape, mybir.dt.from_np(a.dtype), kind="ExternalInput").ap() for n, a in arrays.items()]
    out = nc.dram_tensor("out", (TOK, D), mybir.dt.float32, kind="ExternalOutput").ap()
    o_dram = nc.dram_tensor("o_dram", (TOK, D), mybir.dt.float32, kind="Internal").ap()
    flamingo_kernel(nc, *ins, out, o_dram)
    r = run_bass_kernel_spmd(nc, [arrays], core_ids=[0])
    return np.asarray(r.results[0]["out"]).reshape(B, TQ, D)
```

```python
from contextlib import ExitStack

import numpy as np

import concourse.bass as bass
from concourse import mybir

B, TQ, D = 16, 112, 512
KC = 375
F = 1408
P = 128
DC = D // P
FC = F // P
CK = KC // 3
KEYS = KC + TQ
KPAD = KEYS + 1
PPAD = 4 * CK
TOK = B * TQ
NT = TOK // P
GROUPS = B // 2
PAIRS = NT // 2
EPS = 1e-5
SCALE = float(D) ** -0.5
MAGIC = 12582912.0
WCH = 12
NW = float(F * D)
HCH = [(0, 512), (512, 512), (1024, 384)]


def flamingo_kernel(nc, x, ctxT, ctx, g_xattn, g_ffn, wqT, wkT, wvT, woT, wffn, out, o_dram):
    fp32 = mybir.dt.float32
    f32r = mybir.dt.float32r
    bf16 = mybir.dt.bfloat16
    ALU = mybir.AluOpType
    ACT = mybir.ActivationFunctionType
    AX = mybir.AxisListType.X

    x_b = x.rearrange("(n t) d -> n t d", t=TQ)
    o_b = o_dram.rearrange("(n t) d -> n t d", t=TQ)
    x_t = x.rearrange("(n p) d -> n p d", p=P)
    o_t = o_dram.rearrange("(n p) d -> n p d", p=P)
    y_t = out.rearrange("(n p) d -> n p d", p=P)

    keep = ExitStack()
    with keep:
        def sb(name, shape, dt, stack=keep):
            return stack.enter_context(nc.sbuf_tensor(name, shape, dt))

        def sem(name):
            return keep.enter_context(nc.semaphore(name))

        def sems(name, n=2):
            return [sem(f"{name}{i}") for i in range(n)]

        banks = [keep.enter_context(nc.psum_tensor(f"bank{i}", [P, 512], fp32)) for i in range(8)]

        WQ = sb("ffn_ternary", [P, WCH, F], bf16)
        w2q = WQ[:, 8:12, :].rearrange("p a f -> p (a f)").rearrange("p (c n) -> p c n", n=D)
        wbuf = sb("ffn_raw", [P, 2, F], fp32)
        ident = sb("ident", [P, P], fp32)
        identb = sb("identb", [P, P], bf16)
        ones = sb("ones", [P, P], fp32)
        magic = sb("magic", [P, 2], fp32)
        epsc = sb("epsc", [P, 1], fp32)
        gin = sb("gin", [1, 2], fp32)
        gates = sb("gates", [P, 2], fp32)
        wabs = sb("wabs", [P, WCH], fp32)
        wabs3 = sb("wabs3", [P, 3], fp32)
        wmean = sb("wmean", [P, 3], fp32)
        wscale = sb("wscale", [P, 3], fp32)
        wscur = sb("wscur", [P, 1], fp32)
        bn = sb("bn", [TQ, 2, 6], fp32)
        mv = sb("mv", [TQ, 2, 2], fp32)
        std = sb("std", [TQ, 2], fp32)
        rstd = sb("rstd", [TQ, 2], fp32)
        rowmax = sb("rowmax", [TQ, 2], fp32)
        expbias = sb("expbias", [TQ, 2], fp32)
        rowsum = sb("rowsum", [TQ, 2], fp32)
        rowinv = sb("rowinv", [TQ, 2], fp32)

        half1 = ExitStack()
        wsp = [[sb(f"{w}_{s}", [P, DC, D], f32r, half1) for s in ("hi", "lo")] for w in ("wq", "wk", "wv")]
        kraw = sb("kraw", [P, DC, KC], fp32, half1)
        vraw = sb("vraw", [CK, 3, D], fp32, half1)
        vv = [sb(f"v_{s}", [P, 2, 4, D], f32r, half1) for s in ("hi", "lo")]
        kT = [sb(f"kT_{s}", [P, 2, DC, KPAD], f32r, half1) for s in ("hi", "lo")]
        xT = [sb(f"xT_{s}", [P, DC, 2 * TQ], f32r, half1) for s in ("hi", "lo")]
        qT = [sb(f"qT_{s}", [P, DC, 2 * TQ], f32r, half1) for s in ("hi", "lo")]
        xb = sb("xb", [TQ, 2, D], fp32, half1)
        prob = sb("prob", [TQ, 2, PPAD], fp32, half1)
        pT = [sb(f"pT_{s}", [CK, 2, 4 * TQ], f32r, half1) for s in ("hi", "lo")]
        ob = sb("ob", [TQ, 2, D], fp32, half1)
        half1.close()
        start = ExitStack()
        for w in ("wq", "wk", "wv"):
            for s in ("hi", "lo"):
                sb(f"skip_{w}_{s}", [P, DC, D], f32r, start)
        sb("skip_kraw", [P, DC, KC], fp32, start)
        sb("skip_vraw", [CK, 3, D], fp32, start)
        wraw = sb("wraw", [P, 3, DC, D], fp32, start)
        start.close()

        half2 = ExitStack()
        wo = [sb(f"wo_{s}", [P, DC, D], f32r, half2) for s in ("hi", "lo")]
        x1 = sb("x1", [P, NT, D], fp32, half2)
        ot = sb("ot", [P, 2, D], fp32, half2)
        oT = [sb(f"oT_{s}", [P, 2, DC, P], f32r, half2) for s in ("hi", "lo")]
        bn2 = sb("bn2", [P, NT * 6], fp32, half2)
        mv2 = sb("mv2", [P, NT, 2], fp32, half2)
        std2 = sb("std2", [P, NT], fp32, half2)
        rstd2 = sb("rstd2", [P, NT], fp32, half2)
        nmean2 = sb("nmean2", [P, NT], fp32, half2)
        wdq = sb("wdq", [P, 3], fp32, half2)
        xc = sb("xc", [P, 2, D], fp32, half2)
        xq = sb("xq", [P, 2, D], bf16, half2)
        xqT = sb("xqT", [P, 2, DC, P], bf16, half2)
        hid = sb("hid", [P, 2, F], fp32, half2)
        hq = sb("hq", [P, 2, F], bf16, half2)
        hqT = sb("hqT", [P, 2, FC, P], bf16, half2)
        yb = sb("yb", [P, 2, D], fp32, half2)
        col = {n: sb(n, [P, 2], fp32, half2) for n in ("xamax", "xclip", "xinv", "xmul", "hclip", "hinv", "hmul", "ydq")}
        hamax = sb("hamax", [P, 2, 2], fp32, half2)
        xdq = sb("xdq", [P, 2, 2], fp32, half2)
        half2.close()

        consts = sem("consts")
        g_in, sum_mm, gates_ok = sem("g_in"), sem("sum_mm"), sem("gates_ok")
        pw_in, pw_hi, pw_lo = sems("pw_in", 4), sem("pw_hi"), sem("pw_lo")
        x_in, bn_ok, mv_ok = sems("x_in"), sems("bn_ok"), sem("mv_ok")
        std_ok, rstd_ok, xn_ok = sem("std_ok"), sem("rstd_ok"), sems("xn_ok")
        t_mm, xT_hi, xT_lo = sems("t_mm"), sems("xT_hi_ok"), sems("xT_lo_ok")
        qk_mm, qk_hi, qk_lo = sems("qk_mm"), sems("qk_hi"), sems("qk_lo")
        v_mm, v_hi, v_lo = sems("v_mm"), sems("v_hi_ok"), sems("v_lo_ok")
        k_in, k_hi, k_split = sems("k_in"), sems("k_hi"), sems("k_split")
        v_in, vc_hi, v_split = sems("v_in"), sems("vc_hi"), sems("v_split")
        s_mm, max_ok, bias_ok, exp_ok = sems("s_mm"), sems("max_ok"), sems("bias_ok"), sems("exp_ok")
        inv_ok, pt_mm, pt_hi, pt_lo = sems("inv_ok"), sems("pt_mm"), sems("pt_hi"), sems("pt_lo")
        av_mm, o_ok, o_out = sems("av_mm"), sems("o_ok"), sems("o_out")
        w_in, w_used = sems("w_in"), sems("w_used")
        wabs_ok, wmean_ok, wscale_ok = sem("wabs_ok"), sem("wmean_ok"), sem("wscale_ok")
        wscur_ok, wround_ok = sem("wscur_ok"), sem("wround_ok")
        wo_in, wo_hi_ok, wo_lo_ok = sem("wo_in"), sem("wo_hi_ok"), sem("wo_lo_ok")
        pool_go, dve_go = sem("pool_go"), sem("dve_go")
        ot_in, x1_in = sems("ot_in"), sems("x1_in")
        ot_mm, oT_hi_ok, oT_lo_ok = sems("ot_mm"), sems("oT_hi_ok"), sems("oT_lo_ok")
        pr_mm, x1_ok, bn2_ok = sems("pr_mm"), sems("x1_ok"), sem("bn2_ok")
        mv2_ok, nmean2_ok, std2_ok, rstd2_ok, wdq_ok = (sem(n) for n in ("mv2_ok", "nmean2_ok", "std2_ok", "rstd2_ok", "wdq_ok"))
        xc_ok, xamax_ok, xclip_ok, xinv_ok = sems("xc_ok"), sems("xamax_ok"), sems("xclip_ok"), sems("xinv_ok")
        xmul_ok, xdq_ok, xr_ok, xq_ok = sems("xmul_ok"), sems("xdq_ok"), sems("xr_ok"), sems("xq_ok")
        xq_mm, xqT_ok = sems("xq_mm"), sems("xqT_ok")
        ab_mm, h_ok, silu_ok = sems("ab_mm"), sems("h_ok"), sems("silu_ok")
        hamax_ok, hclip_ok, hinv_ok, hmul_ok, ydq_ok = (sems(n) for n in ("hamax_ok", "hclip_ok", "hinv_ok", "hmul_ok", "ydq_ok"))
        hr_ok, hq_ok, h_mm, hT_a, hT_b = sems("hr_ok"), sems("hq_ok"), sems("h_mm"), sems("hT_a"), sems("hT_b")
        w2_mm, y_ok, y_out = sems("w2_mm"), sems("y_ok"), sems("y_out")

        X1_TILES = ((0, 2), (2, NT))
        HALVES = (slice(0, 6 * P), slice(6 * P, F))
        HI, LO = 0, 1
        PW = [(0, slice(0, D // 2)), (0, slice(D // 2, D)), (1, slice(0, D)), (2, slice(0, D))]
        PASSES = [(HI, HI), (HI, LO), (LO, HI)]
        Q_BANK, R_BANK, S_BANK = banks[0:2], banks[2:4], banks[4:6]
        PT_BANK, AV_BANK = banks[6], banks[7]

        XQ_PS = banks[4][:, 0:2 * P].bitcast(bf16).rearrange("p (c t) -> p c t", c=DC)
        H_PS = [banks[5][:, 0:4 * P].bitcast(bf16).rearrange("p (c t) -> p c t", c=8),
                banks[6][:, 0:3 * P // 2].bitcast(bf16).rearrange("p (c t) -> p c t", c=3)]

        def k_new(bank):
            return bank[:, 0:4 * TQ].rearrange("p (e u t) -> p u e t", e=2, u=2)

        def two(bank):
            return bank[:, 0:4 * TQ].rearrange("p (e t) -> p e t", e=2)

        def four(bank, n):
            return bank[:, 0:4 * n].rearrange("p (c t) -> p c t", c=4)

        def fr(ap):
            return ap.bitcast(fp32)

        def first_half_over(eng):
            for u in range(2):
                eng.wait_ge(o_ok[u], GROUPS)
                eng.wait_ge(o_out[u], 16 * GROUPS)

        def bank_turn(u, j):
            return (3 * u + j) % 2, (3 * u + j) // 2

        block = keep.enter_context(nc.Block())

        @block.sync
        def _(eng):
            def load_x(g, u):
                eng.wait_ge(t_mm[u], g)
                eng.dma_start(xb[:, u, :], x_b[bass.ds(2 * g + u, 1), :, :].rearrange("a t d -> (a t) d")).then_inc(x_in[u], 16)

            def load_k(g, u):
                if not (isinstance(g, int) and g == 0 and u == 0):
                    eng.wait_ge(k_split[1 - u], g + u)
                eng.dma_start(kraw[:, :, :], ctxT[bass.ds(2 * g + u, 1), :, :, :].rearrange("a p c k -> (a p) c k")).then_inc(k_in[u], 16)

            def load_v(g, u):
                if not (isinstance(g, int) and g == 0 and u == 0):
                    eng.wait_ge(v_split[1 - u], g + u)
                eng.dma_start(vraw[:, :, :], ctx[bass.ds(2 * g + u, 1), :, :, :].rearrange("a p c d -> (a p) c d")).then_inc(v_in[u], 16)

            def load_w(chunk, turn, j):
                eng.wait_ge(w_used[j % 2], turn + j // 2)
                eng.dma_start(wbuf[:, j % 2, :], wffn[bass.ds(chunk + j, 1), :, :].rearrange("a p f -> (a p) f")).then_inc(w_in[j % 2], 16)

            def store_o(g, u):
                eng.wait_ge(o_ok[u], g + 1)
                eng.dma_start(o_b[bass.ds(2 * g + u, 1), :, :].rearrange("a t d -> (a t) d"), ob[:, u, :]).then_inc(o_out[u], 16)

            def group(g, w=None, more=True, first=False):
                if w:
                    load_w(*w, 0)
                load_v(g, 1)
                if not first:
                    store_o(g - 1, 0)
                    store_o(g - 1, 1)
                if w:
                    load_w(*w, 1)
                load_k(g + 1, 0)
                if w:
                    load_w(*w, 2)
                load_v(g + 1, 0)
                if w:
                    load_w(*w, 3)
                load_k(g + 1, 1)
                if more:
                    load_x(g + 2, 0)
                    load_x(g + 2, 1)

            for u in range(2):
                eng.dma_start(xb[:, u, :], x_b[u, :, :]).then_inc(x_in[u], 16)
            for n, e in enumerate((slice(0, D // 2), slice(D // 2, D))):
                eng.dma_start(wraw[:, 0, :, e], wqT[:, :, e]).then_inc(pw_in[n], 16)
            eng.dma_start(gin[0:1, 0:1], g_xattn.rearrange("(a b) -> a b", a=1)).then_inc(g_in, 16)
            eng.dma_start(gin[0:1, 1:2], g_ffn.rearrange("(a b) -> a b", a=1)).then_inc(g_in, 16)
            eng.dma_start(wraw[:, 1, :, :], wkT).then_inc(pw_in[2], 16)
            load_k(0, 0)
            eng.dma_start(wraw[:, 2, :, :], wvT).then_inc(pw_in[3], 16)
            load_v(0, 0)
            load_x(1, 0)
            load_x(1, 1)
            load_k(0, 1)
            group(0, (0, 0), first=True)
            with eng.Fori(1, 3) as g:
                group(g, (4 * g, 2 * g))
            group(3)
            with eng.Fori(4, 6) as g:
                group(g, (4 * g - 16, 2 * g - 2))
            group(6, (8, 10), more=False)
            load_v(7, 1)
            store_o(6, 0)
            store_o(6, 1)
            for s in w_used:
                eng.wait_ge(s, 12)
            eng.dma_start(wbuf[:, :, :].rearrange("p a f -> p (a f)")[:, 0:DC * D].rearrange("p (c n) -> p c n", c=DC), woT).then_inc(wo_in, 16)
            for u in range(2):
                eng.wait_ge(qk_mm[u], 2 * GROUPS)
                eng.wait_ge(v_mm[u], GROUPS)
            def load_o(i, u):
                eng.wait_ge(ot_mm[u], i)
                eng.dma_start(ot[:, u, :], o_t[bass.ds(2 * i + u, 1), :, :].rearrange("a p d -> (a p) d")).then_inc(ot_in[u], 16)

            for u in range(2):
                eng.wait_ge(o_out[u], 16 * (GROUPS - 1))
                load_o(0, u)
            for n, (a, b) in enumerate(X1_TILES):
                eng.dma_start(x1[:, a:b, :], x_t[a:b, :, :].rearrange("n p d -> p n d")).then_inc(x1_in[n], 16)
            store_o(7, 0)
            store_o(7, 1)
            with eng.Fori(1, PAIRS - 1) as i:
                load_o(i, 0)
                load_o(i, 1)
            for u in range(2):
                eng.wait_ge(o_out[u], 16 * GROUPS)
                load_o(PAIRS - 1, u)
            with eng.Fori(0, PAIRS) as i:
                for u in range(2):
                    eng.wait_ge(y_ok[u], i + 1)
                    eng.dma_start(y_t[bass.ds(2 * i + u, 1), :, :].rearrange("a p d -> (a p) d"), yb[:, u, :]).then_inc(y_out[u], 16)
            for u in range(2):
                eng.wait_ge(y_out[u], 16 * PAIRS)

        @block.gpsimd
        def _(eng):
            eng.memset(ident[:, :], 0.0).then_inc(consts, 1)
            eng.memset(identb[:, :], 0.0).then_inc(consts, 1)
            eng.memset(ones[:, :], 1.0).then_inc(consts, 1)
            eng.memset(magic[:, 0:1], MAGIC).then_inc(consts, 1)
            eng.memset(magic[:, 1:2], -MAGIC).then_inc(consts, 1)
            eng.memset(epsc[:, :], EPS).then_inc(consts, 1)
            for half in kT:
                eng.memset(half[:, :, :, KEYS:KPAD].bitcast(fp32), 0.0).then_inc(consts, 1)
            eng.memset(prob[:, :, KEYS:PPAD], 0.0).then_inc(consts, 1)
            eng.wait_ge(consts, 9)
            for m in (ident, identb):
                eng.affine_select(out=m[:, :], in_=m[:, :], compare_op=ALU.not_equal, fill=1.0,
                                  base=0, pattern=[[-1, P]], channel_multiplier=1).then_inc(consts, 1)
            def split(g, u):
                eng.wait_ge(k_in[u], 16 * g + 16)
                eng.wait_ge(s_mm[u], g)
                eng.sem_inc(pool_go, 1)
                eng.tensor_scalar(kT[HI][:, u, :, 0:KC], kraw[:, :, :], 1.0, 0.0, ALU.mult, ALU.add).then_inc(k_hi[u], 1)
                eng.wait_ge(k_hi[u], g + 1)
                eng.tensor_tensor(kT[LO][:, u, :, 0:KC], kraw[:, :, :], fr(kT[HI][:, u, :, 0:KC]), ALU.subtract).then_inc(k_split[u], 1)
                eng.wait_ge(pw_lo, len(PW))
                eng.wait_ge(v_in[u], 16 * g + 16)
                eng.wait_ge(av_mm[u], g)
                eng.sem_inc(pool_go, 1)
                eng.tensor_scalar(vv[HI][0:CK, u, 0:3, :], vraw[:, :, :], 1.0, 0.0, ALU.mult, ALU.add).then_inc(vc_hi[u], 1)
                eng.wait_ge(vc_hi[u], g + 1)
                eng.tensor_tensor(vv[LO][0:CK, u, 0:3, :], vraw[:, :, :], fr(vv[HI][0:CK, u, 0:3, :]), ALU.subtract).then_inc(v_split[u], 1)

            for u in range(2):
                split(0, u)
            with eng.Fori(1, GROUPS) as g:
                for u in range(2):
                    split(g, u)

            def quant_x(i, u):
                eng.wait_ge(xmul_ok[u], i + 1)
                eng.sem_inc(pool_go, 1)
                eng.tensor_scalar(xc[:, u, :], xc[:, u, :], col["xmul"][:, u:u + 1], MAGIC, ALU.mult, ALU.add).then_inc(xr_ok[u], 1)
                eng.wait_ge(xr_ok[u], i + 1)
                eng.wait_ge(xq_mm[u], i)
                eng.sem_inc(pool_go, 1)
                eng.tensor_scalar(xq[:, u, :], xc[:, u, :], -MAGIC, 1.0, ALU.add, ALU.mult).then_inc(xq_ok[u], 1)

            def quant_h(i, u):
                for n, a in enumerate(HALVES):
                    eng.wait_ge(hr_ok[u], 2 * i + n + 1)
                    eng.wait_ge(h_mm[u], i)
                    eng.sem_inc(pool_go, 1)
                    eng.tensor_scalar(hq[:, u, a], hid[:, u, a], -MAGIC, 1.0, ALU.add, ALU.mult).then_inc(hq_ok[u], 1)

            for u in range(2):
                quant_x(0, u)
            for u in range(2):
                quant_h(0, u)
                quant_x(1, u)
            with eng.Fori(1, PAIRS - 1) as i:
                for u in range(2):
                    quant_h(i, u)
                    quant_x(i + 1, u)
            for u in range(2):
                quant_h(PAIRS - 1, u)

        @block.scalar
        def _(act):
            def std_of(g):
                act.wait_ge(mv_ok, 2 * g + 2)
                nc.scalar.activation(std[:, :], mv[:, :, 1], ACT.Sqrt, bias=epsc[0:TQ, 0:1]).then_inc(std_ok, 1)

            def x_hi(g, u):
                act.wait_ge(t_mm[u], g + 1)
                act.wait_ge(v_mm[0], g)
                act.wait_ge(v_mm[1], g)
                nc.scalar.copy(xT[HI][:, :, u * TQ:(u + 1) * TQ], four(R_BANK[u], TQ)).then_inc(xT_hi[u], 1)

            def qk(g, j):
                act.wait_ge(qk_mm[j % 2], 2 * g + j // 2 + 1)
                if j == 0:
                    for u in range(2):
                        act.wait_ge(s_mm[u], g)
                if j < 2:
                    nc.scalar.copy(qT[HI][:, 2 * j:2 * j + 2, :], two(Q_BANK[j % 2])).then_inc(qk_hi[j % 2], 1)
                else:
                    e = 2 * (j - 2)
                    nc.scalar.copy(kT[HI][:, :, e:e + 2, KC:KEYS], k_new(Q_BANK[j % 2])).then_inc(qk_hi[j % 2], 1)

            def v(g, u):
                act.wait_ge(v_mm[u], g + 1)
                act.wait_ge(av_mm[u], g)
                act.wait_ge(pw_lo, len(PW))
                nc.scalar.copy(vv[HI][0:TQ, u, 3, :], R_BANK[u][0:TQ, :]).then_inc(v_hi[u], 1)

            def exp(g, u):
                act.wait_ge(bias_ok[u], g + 1)
                act.wait_ge(pt_mm[u], g)
                nc.scalar.activation(prob[:, u, 0:KEYS], S_BANK[u][0:TQ, 0:KEYS], ACT.Exp, bias=expbias[:, u:u + 1],
                                     scale=SCALE, accum_out=rowsum[:, u:u + 1]).then_inc(exp_ok[u], 1)

            def pt(g, u):
                act.wait_ge(pt_mm[u], g + 1)
                act.wait_ge(av_mm[u], g)
                nc.scalar.copy(pT[HI][:, u, :], PT_BANK[0:CK, 0:4 * TQ]).then_inc(pt_hi[u], 1)

            def o(g, u):
                act.wait_ge(av_mm[u], g + 1)
                act.wait_ge(inv_ok[u], g + 1)
                act.wait_ge(o_out[u], 16 * g)
                nc.scalar.activation(ob[:, u, :], AV_BANK[0:TQ, :], ACT.Copy, scale=rowinv[:, u:u + 1]).then_inc(o_ok[u], 1)

            def round_w(g, j):
                s = j % 2
                act.wait_ge(w_in[s], 16 * (2 * g - 2 + j // 2) + 16)
                nc.scalar.activation(wbuf[:, s, :], wbuf[:, s, :], ACT.Identity, bias=magic[:, 0:1],
                                     scale=wscur[:, 0:1]).then_inc(wround_ok, 1)

            def sign_w(g, j):
                s = j % 2
                act.wait_ge(wround_ok, 4 * g - 16 + j + 1)
                nc.scalar.activation(WQ[:, bass.ds(4 * g - 16 + j, 1), :].rearrange("p a f -> p (a f)"), wbuf[:, s, :],
                                     ACT.Sign, bias=magic[:, 1:2]).then_inc(w_used[s], 1)

            def group(g, w=False, last=False):
                if w:
                    act.wait_ge(wscale_ok, 1)
                    act.wait_ge(w_used[1], 2 * g - 2)
                    nc.scalar.copy(wscur[:, 0:1], wscale[:, bass.ds(g - 4, 1)]).then_inc(wscur_ok, 1)
                    act.wait_ge(wscur_ok, g - 3)
                qk(g, 1)
                if w:
                    round_w(g, 0)
                qk(g, 2)
                if w:
                    sign_w(g, 0)
                qk(g, 3)
                if not last:
                    std_of(g + 1)
                v(g, 0)
                if w:
                    round_w(g, 1)
                exp(g, 0)
                if w:
                    sign_w(g, 1)
                v(g, 1)
                pt(g, 0)
                if w:
                    round_w(g, 2)
                exp(g, 1)
                if not last:
                    x_hi(g + 1, 0)
                    x_hi(g + 1, 1)
                if w:
                    sign_w(g, 2)
                o(g, 0)
                pt(g, 1)
                if w:
                    round_w(g, 3)
                if last:
                    act.wait_ge(wo_in, 16)
                    for s in qk_mm:
                        act.wait_ge(s, 2 * GROUPS)
                    nc.scalar.copy(wo[HI][:, :, :], raw_wo).then_inc(wo_hi_ok, 1)
                else:
                    qk(g + 1, 0)
                o(g, 1)
                if w:
                    sign_w(g, 3)

            raw_wo = wbuf[:, :, :].rearrange("p a f -> p (a f)")[:, 0:DC * D].rearrange("p (c n) -> p c n", c=DC)
            act.wait_ge(consts, 11)
            std_of(0)
            for n, (i, e) in enumerate(PW):
                act.wait_ge(pw_in[n], 16)
                nc.scalar.copy(wsp[i][HI][:, :, e], wraw[:, i, :, e]).then_inc(pw_hi, 1)
                if n == 0:
                    x_hi(0, 0)
                    x_hi(0, 1)
            act.wait_ge(sum_mm, 1)
            nc.scalar.activation(gates[:, :], AV_BANK[:, 0:2], ACT.Tanh).then_inc(gates_ok, 1)
            qk(0, 0)
            group(0)
            with act.Fori(1, 3) as g:
                group(g)
            group(3)
            with act.Fori(4, 7) as g:
                group(g, w=True)
            group(7, last=True)

            for u in range(2):
                act.wait_ge(k_split[u], GROUPS)
                act.wait_ge(v_split[u], GROUPS)

            def oT_high(i, u):
                act.wait_ge(ot_mm[u], i + 1)
                act.wait_ge(pr_mm[u], i)
                nc.scalar.copy(oT[HI][:, u, :, :], four(banks[u], P)).then_inc(oT_hi_ok[u], 1)

            def deviations(first, last):
                act.wait_ge(mv2_ok, last)
                nc.scalar.activation(std2[:, first:last], mv2[:, first:last, 1], ACT.Sqrt, bias=epsc[:, 0:1]).then_inc(std2_ok, 1)

            def center(i, u):
                act.wait_ge(xq_ok[u], i)
                nc.scalar.activation(xc[:, u, :], x1[:, bass.ds(2 * i + u, 1), :].rearrange("p a d -> p (a d)"),
                                     ACT.Identity, bias=nmean2[:, bass.ds(2 * i + u, 1)]).then_inc(xc_ok[u], 1)

            def silu(i, u, j):
                c, n = HCH[j]
                k, turn = bank_turn(u, j)
                act.wait_ge(ab_mm[k], 3 * i + turn + 1)
                if j == 0:
                    act.wait_ge(xdq_ok[u], i + 1)
                    act.wait_ge(hq_ok[u], 2 * i)
                nc.scalar.activation(hid[:, u, c:c + n], banks[k][:, 0:n], ACT.Silu,
                                     scale=xdq[:, u, 0:1]).then_inc(silu_ok[u], 1)

            def xqT_copy(i, u):
                act.wait_ge(xq_mm[u], i + 1)
                nc.scalar.copy(xqT[:, u, :, :], XQ_PS).then_inc(xqT_ok[u], 1)

            def hT_copy(i, u):
                act.wait_ge(h_mm[u], i + 1)
                act.wait_ge(w2_mm[u], i)
                nc.scalar.copy(hqT[:, u, 0:8, :], H_PS[0]).then_inc(hT_a[u], 1)

            def round_h(i, u):
                act.wait_ge(hmul_ok[u], i + 1)
                for a in HALVES:
                    nc.scalar.activation(hid[:, u, a], hid[:, u, a], ACT.Identity, bias=magic[:, 0:1],
                                         scale=col["hmul"][:, u:u + 1]).then_inc(hr_ok[u], 1)

            def tile(i, u, first=False, last=False, more=True):
                silu(i, u, 0)
                silu(i, u, 1)
                if not first:
                    hT_copy(i + u - 1, 1 - u)
                silu(i, u, 2)
                if not last:
                    xqT_copy(i + u, 1 - u)
                if more:
                    center(i + 1, u)
                round_h(i, u)

            for i, u in ((0, 0), (0, 1), (1, 0)):
                oT_high(i, u)
            first_half_over(act)
            deviations(0, 2)
            oT_high(1, 1)
            with act.Fori(2, 4) as i:
                oT_high(i, 0)
                oT_high(i, 1)
            act.wait_ge(nmean2_ok, 1)
            center(0, 0)
            center(0, 1)
            with act.Fori(4, PAIRS) as i:
                oT_high(i, 0)
                oT_high(i, 1)
            xqT_copy(0, 0)
            deviations(2, NT)
            act.wait_ge(nmean2_ok, 2)
            tile(0, 0, first=True)
            tile(0, 1)
            with act.Fori(1, PAIRS - 1) as i:
                tile(i, 0)
                tile(i, 1)
            tile(PAIRS - 1, 0, more=False)
            tile(PAIRS - 1, 1, last=True, more=False)
            hT_copy(PAIRS - 1, 1)

        @block.vector
        def _(dve):
            V = nc.vector

            def stats(g):
                for u in range(2):
                    dve.wait_ge(x_in[u], 16 * g + 16)
                    V.bn_stats(bn[:, u, :], xb[:, u, :]).then_inc(bn_ok[u], 1)
                    dve.wait_ge(bn_ok[u], g + 1)
                    dve.sem_inc(dve_go, 1)
                    V.bn_aggr(mv[:, u, :], bn[:, u, :]).then_inc(mv_ok, 1)

            def normalise(g):
                dve.wait_ge(std_ok, g + 1)
                V.reciprocal(rstd[:, :], std[:, :]).then_inc(rstd_ok, 1)
                dve.wait_ge(rstd_ok, g + 1)
                for u in range(2):
                    V.tensor_scalar(xb[:, u, :], xb[:, u, :], mv[:, u, 0:1], rstd[:, u:u + 1],
                                    ALU.subtract, ALU.mult).then_inc(xn_ok[u], 1)

            def x_lo(g, u):
                dve.wait_ge(xT_hi[u], g + 1)
                d = slice(u * TQ, (u + 1) * TQ)
                V.tensor_tensor(xT[LO][:, :, d], four(R_BANK[u], TQ), fr(xT[HI][:, :, d]), ALU.subtract).then_inc(xT_lo[u], 1)

            def qk(g, j):
                dve.wait_ge(qk_hi[j % 2], 2 * g + j // 2 + 1)
                if j < 2:
                    d = slice(2 * j, 2 * j + 2)
                    V.tensor_tensor(qT[LO][:, d, :], two(Q_BANK[j % 2]), fr(qT[HI][:, d, :]), ALU.subtract).then_inc(qk_lo[j % 2], 1)
                else:
                    e = 2 * (j - 2)
                    V.tensor_tensor(kT[LO][:, :, e:e + 2, KC:KEYS], k_new(Q_BANK[j % 2]),
                                    fr(kT[HI][:, :, e:e + 2, KC:KEYS]), ALU.subtract).then_inc(qk_lo[j % 2], 1)

            def v(g, u):
                dve.wait_ge(v_hi[u], g + 1)
                V.tensor_tensor(vv[LO][0:TQ, u, 3, :], R_BANK[u][0:TQ, :], fr(vv[HI][0:TQ, u, 3, :]),
                                ALU.subtract).then_inc(v_lo[u], 1)

            def rowmaxima(g, u):
                dve.wait_ge(s_mm[u], g + 1)
                V.tensor_reduce(rowmax[:, u:u + 1], S_BANK[u][0:TQ, 0:KEYS], AX, ALU.max).then_inc(max_ok[u], 1)
                dve.wait_ge(max_ok[u], g + 1)
                dve.wait_ge(exp_ok[u], g)
                V.tensor_scalar(expbias[:, u:u + 1], rowmax[:, u:u + 1], -SCALE, None, ALU.mult).then_inc(bias_ok[u], 1)

            def pt(g, u):
                dve.wait_ge(pt_hi[u], g + 1)
                V.tensor_tensor(pT[LO][:, u, :], PT_BANK[0:CK, 0:4 * TQ], fr(pT[HI][:, u, :]), ALU.subtract).then_inc(pt_lo[u], 1)
                dve.wait_ge(exp_ok[u], g + 1)
                dve.wait_ge(o_ok[u], g)
                V.reciprocal(rowinv[:, u:u + 1], rowsum[:, u:u + 1]).then_inc(inv_ok[u], 1)

            def magnitudes(g, j):
                dve.wait_ge(w_in[j % 2], 16 * (2 * g + j // 2) + 16)
                V.tensor_reduce(wabs[:, bass.ds(4 * g + j, 1)], wbuf[:, j % 2, :], AX, ALU.add,
                                apply_absolute_value=True).then_inc(w_used[j % 2], 1)

            def group(g, w=False, scales=False, first=False, last=False):
                qk(g, 1)
                if w and not first:
                    magnitudes(g, 0)
                qk(g, 2)
                if not last:
                    stats(g + 1)
                qk(g, 3)
                if w and not first:
                    magnitudes(g, 1)
                if scales:
                    for s in w_used:
                        dve.wait_ge(s, 6)
                    V.tensor_reduce(wabs3[:, :], wabs[:, :].rearrange("p (m c) -> p m c", c=4), AX, ALU.add).then_inc(wabs_ok, 1)
                v(g, 0)
                rowmaxima(g, 0)
                if w:
                    magnitudes(g, 0 if first else 2)
                v(g, 1)
                if not last:
                    normalise(g + 1)
                pt(g, 0)
                rowmaxima(g, 1)
                if not last:
                    x_lo(g + 1, 0)
                    x_lo(g + 1, 1)
                if w:
                    magnitudes(g, 1 if first else 3)
                pt(g, 1)
                if scales:
                    dve.wait_ge(sum_mm, 2)
                    V.tensor_scalar(wmean[:, :], AV_BANK[:, 0:3], 1.0 / NW, EPS, ALU.mult, ALU.max).then_inc(wmean_ok, 1)
                    dve.wait_ge(wmean_ok, 1)
                    V.reciprocal(wscale[:, :], wmean[:, :]).then_inc(wscale_ok, 1)
                if last:
                    dve.wait_ge(wo_hi_ok, 1)
                    V.tensor_tensor(wo[LO][:, :, :], raw_wo, fr(wo[HI][:, :, :]), ALU.subtract).then_inc(wo_lo_ok, 1)
                else:
                    qk(g + 1, 0)
                if first:
                    magnitudes(g, 2)
                    magnitudes(g, 3)

            raw_wo = wbuf[:, :, :].rearrange("p a f -> p (a f)")[:, 0:DC * D].rearrange("p (c n) -> p c n", c=DC)
            stats(0)
            normalise(0)
            for n, (i, e) in enumerate(PW):
                dve.wait_ge(pw_hi, n + 1)
                V.tensor_tensor(wsp[i][LO][:, :, e], wraw[:, i, :, e], fr(wsp[i][HI][:, :, e]), ALU.subtract).then_inc(pw_lo, 1)
                if n == 0:
                    x_lo(0, 0)
                    x_lo(0, 1)
            qk(0, 0)
            group(0, w=True, first=True)
            with dve.Fori(1, 3) as g:
                group(g, w=True)
            group(3, scales=True)
            with dve.Fori(4, 7) as g:
                group(g)
            group(7, last=True)

            for u in range(2):
                dve.wait_ge(k_split[u], GROUPS)
                dve.wait_ge(v_split[u], GROUPS)
            dve.wait_ge(gates_ok, 1)
            dve.wait_ge(x1_in[0], 16)

            def oT_low(i, u):
                dve.wait_ge(oT_hi_ok[u], i + 1)
                V.tensor_tensor(oT[LO][:, u, :, :], four(banks[u], P), fr(oT[HI][:, u, :, :]), ALU.subtract).then_inc(oT_lo_ok[u], 1)

            def add(i, u):
                dve.wait_ge(pr_mm[u], i + 1)
                t = x1[:, bass.ds(2 * i + u, 1), :].rearrange("p a d -> p (a d)")
                V.scalar_tensor_tensor(out=t, in0=banks[2 + u][:, :], scalar=gates[:, 0:1], in1=t,
                                       op0=ALU.mult, op1=ALU.add).then_inc(x1_ok[u], 1)
                dve.wait_ge(x1_ok[u], i + 1)
                V.bn_stats(bn2[:, bass.ds(12 * i + 6 * u, 6)], t).then_inc(bn2_ok, 1)

            def moments(first, last):
                dve.wait_ge(bn2_ok, last)
                for t in range(first, last):
                    V.bn_aggr(mv2[:, t, :], bn2[:, 6 * t:6 * t + 6]).then_inc(mv2_ok, 1)
                dve.wait_ge(mv2_ok, last)
                V.tensor_scalar(nmean2[:, first:last], mv2[:, first:last, 0], -1.0, None, ALU.mult).then_inc(nmean2_ok, 1)

            def deviations(first, last, n):
                dve.wait_ge(std2_ok, n)
                V.reciprocal(rstd2[:, first:last], std2[:, first:last]).then_inc(rstd2_ok, 1)
                dve.wait_ge(rstd2_ok, n)

            def pair(i):
                oT_low(i, 1)
                add(i, 0)
                oT_low(i + 1, 0)
                add(i, 1)

            c = {n: (lambda a: (lambda u: a[:, u:u + 1]))(a) for n, a in col.items()}

            def x_scale(i, u):
                r = rstd2[:, bass.ds(2 * i + u, 1)]
                dve.wait_ge(xc_ok[u], i + 1)
                V.tensor_reduce(c["xamax"](u), xc[:, u, :], AX, ALU.max, apply_absolute_value=True).then_inc(xamax_ok[u], 1)
                dve.wait_ge(xamax_ok[u], i + 1)
                V.tensor_scalar(c["xclip"](u), c["xamax"](u), r, EPS, ALU.mult, ALU.max).then_inc(xclip_ok[u], 1)
                dve.wait_ge(xclip_ok[u], i + 1)
                V.reciprocal(c["xinv"](u), c["xclip"](u)).then_inc(xinv_ok[u], 1)
                V.tensor_scalar(xdq[:, u, :], wdq[:, 0:2], c["xclip"](u), None, ALU.mult).then_inc(xdq_ok[u], 1)
                dve.wait_ge(xinv_ok[u], i + 1)
                V.tensor_scalar(c["xmul"](u), c["xinv"](u), 127.0, r, ALU.mult, ALU.mult).then_inc(xmul_ok[u], 1)

            def hidden(i, u, js):
                for j in js:
                    a, n = HCH[j]
                    k, turn = bank_turn(u, j)
                    dve.wait_ge(silu_ok[u], 3 * i + j + 1)
                    dve.wait_ge(xdq_ok[u], i + 1)
                    V.scalar_tensor_tensor(out=hid[:, u, a:a + n], in0=banks[2 + k][:, 0:n], scalar=xdq[:, u, 1:2],
                                           in1=hid[:, u, a:a + n], op0=ALU.mult, op1=ALU.mult).then_inc(h_ok[k], 1)

            def h_max(i, u, part):
                need = ((1, 1), (2, 1))[part] if u == 0 else ((3, 2), (3, 3))[part]
                for k in range(2):
                    dve.wait_ge(h_ok[k], 3 * i + need[k])
                a = slice(0, 1024) if part == 0 else slice(1024, F)
                V.tensor_reduce(hamax[:, u, part:part + 1], hid[:, u, a], AX, ALU.max, apply_absolute_value=True).then_inc(hamax_ok[u], 1)

            def h_scale(i, u):
                dve.wait_ge(hamax_ok[u], 2 * i + 2)
                V.tensor_scalar(c["hclip"](u), hamax[:, u, 0:1], hamax[:, u, 1:2], EPS, ALU.max, ALU.max).then_inc(hclip_ok[u], 1)
                dve.wait_ge(hclip_ok[u], i + 1)
                V.reciprocal(c["hinv"](u), c["hclip"](u)).then_inc(hinv_ok[u], 1)
                dve.wait_ge(hinv_ok[u], i + 1)
                V.tensor_scalar(c["hmul"](u), c["hinv"](u), 127.0, None, ALU.mult).then_inc(hmul_ok[u], 1)
                V.tensor_scalar(c["ydq"](u), c["hclip"](u), wdq[:, 2:3], None, ALU.mult).then_inc(ydq_ok[u], 1)

            def hT_copy(i, u):
                dve.wait_ge(h_mm[u], i + 1)
                dve.wait_ge(w2_mm[u], i)
                V.tensor_copy(hqT[:, u, 8:FC, :], H_PS[1]).then_inc(hT_b[u], 1)

            def result(i, u):
                dve.wait_ge(w2_mm[u], i + 1)
                dve.wait_ge(ydq_ok[u], i + 1)
                dve.wait_ge(y_out[u], 16 * i)
                V.scalar_tensor_tensor(out=yb[:, u, :], in0=banks[7][:, :], scalar=c["ydq"](u),
                                       in1=x1[:, bass.ds(2 * i + u, 1), :].rearrange("p a d -> p (a d)"),
                                       op0=ALU.mult, op1=ALU.add).then_inc(y_ok[u], 1)

            def tile(i, u, first=False, more=True):
                hidden(i, u, (0, 1))
                if not first:
                    hT_copy(i + u - 1, 1 - u)
                h_max(i, u, 0)
                hidden(i, u, (2,))
                h_max(i, u, 1)
                h_scale(i, u)
                if more:
                    x_scale(i + 1, u)
                if not first:
                    result(i + u - 1, 1 - u)

            oT_low(0, 0)
            pair(0)
            first_half_over(dve)
            V.tensor_scalar(wdq[:, 0:2], wmean[:, 0:2], 1.0 / 127.0, None, ALU.mult).then_inc(wdq_ok, 1)
            V.tensor_scalar(wdq[:, 2:3], wmean[:, 2:3], 1.0 / 127.0, gates[:, 1:2], ALU.mult, ALU.mult).then_inc(wdq_ok, 1)
            dve.wait_ge(wdq_ok, 2)
            moments(0, 2)
            dve.wait_ge(x1_in[1], 16)
            with dve.Fori(1, 3) as i:
                pair(i)
            deviations(0, 2, 1)
            pair(3)
            x_scale(0, 0)
            x_scale(0, 1)
            with dve.Fori(4, PAIRS - 1) as i:
                pair(i)
            oT_low(PAIRS - 1, 1)
            add(PAIRS - 1, 0)
            add(PAIRS - 1, 1)
            moments(2, NT)
            deviations(2, NT, 2)
            tile(0, 0, first=True)
            tile(0, 1)
            with dve.Fori(1, PAIRS - 1) as i:
                tile(i, 0)
                tile(i, 1)
            tile(PAIRS - 1, 0, more=False)
            tile(PAIRS - 1, 1, more=False)
            hT_copy(PAIRS - 1, 1)
            result(PAIRS - 1, 1)

        @block.tensor
        def _(pe):
            def products(dst, pairs):
                for n, (a, b) in enumerate(pairs):
                    ins = nc.tensor.matmul(dst, a, b, start=(n == 0), stop=(n == len(pairs) - 1))
                return ins

            def transpose_x(g, u):
                pe.wait_ge(xn_ok[u], g + 1)
                pe.wait_ge(v_lo[u], g)
                for c in range(DC):
                    ins = nc.tensor.transpose(R_BANK[u][:, c * TQ:(c + 1) * TQ], xb[:, u, c * P:(c + 1) * P], ident[0:TQ, 0:TQ])
                ins.then_inc(t_mm[u], 1)

            def qk(g, js):
                for u in range(2):
                    pe.wait_ge(xT_lo[u], g + 1)
                for j in js:
                    pe.wait_ge(pw_lo, min(j + 1, 3))
                    pe.wait_ge(qk_lo[j % 2], 2 * g + j // 2)
                    w = wsp[j // 2]
                    for e in range(2):
                        o = 2 * (j % 2) + e
                        ins = products(Q_BANK[j % 2][:, e * 2 * TQ:(e + 1) * 2 * TQ],
                                       [(w[a][:, c, o * P:(o + 1) * P], xT[b][:, c, :]) for c in range(DC) for a, b in PASSES])
                    ins.then_inc(qk_mm[j % 2], 1)

            def v(g, u):
                pe.wait_ge(pw_lo, len(PW))
                products(R_BANK[u][0:TQ, :], [(xT[a][:, c, u * TQ:(u + 1) * TQ], wsp[2][b][:, c, :])
                                              for c in range(DC) for a, b in PASSES]).then_inc(v_mm[u], 1)

            def scores(g, u):
                for s in qk_lo:
                    pe.wait_ge(s, 2 * g + 2)
                pe.wait_ge(k_split[u], g + 1)
                pe.wait_ge(exp_ok[u], g)
                products(S_BANK[u][0:TQ, 0:KPAD], [(qT[a][:, c, u * TQ:(u + 1) * TQ], kT[b][:, u, c, :])
                                                   for c in range(DC) for a, b in PASSES]).then_inc(s_mm[u], 1)

            def transpose_p(g, u):
                pe.wait_ge(exp_ok[u], g + 1)
                pe.wait_ge(pt_lo[1 - u], g + u)
                for c in range(4):
                    ins = nc.tensor.transpose(PT_BANK[0:CK, c * TQ:(c + 1) * TQ], prob[:, u, c * CK:(c + 1) * CK], ident[0:TQ, 0:TQ])
                ins.then_inc(pt_mm[u], 1)

            def values(g, u):
                pe.wait_ge(pt_lo[u], g + 1)
                pe.wait_ge(v_lo[u], g + 1)
                pe.wait_ge(v_split[u], g + 1)
                pe.wait_ge(o_ok[1 - u], g + u)
                n = [CK, CK, CK, TQ]
                products(AV_BANK[0:TQ, :], [(pT[a][0:n[c], u, c * TQ:(c + 1) * TQ], vv[b][0:n[c], u, c, :])
                                            for c in range(4) for a, b in PASSES]).then_inc(av_mm[u], 1)

            def group(g, first=False, scales=False, last=False):
                qk(g, (1, 2, 3))
                v(g, 0)
                scores(g, 0)
                v(g, 1)
                transpose_p(g, 0)
                scores(g, 1)
                if not last:
                    transpose_x(g + 1, 0)
                    transpose_x(g + 1, 1)
                if first:
                    pe.wait_ge(gates_ok, 1)
                values(g, 0)
                transpose_p(g, 1)
                if not last:
                    qk(g + 1, (0,))
                if scales:
                    pe.wait_ge(wabs_ok, 1)
                    pe.wait_ge(o_ok[0], g + 1)
                    nc.tensor.matmul(AV_BANK[:, 0:3], ones[:, :], wabs3[:, :], start=True, stop=True).then_inc(sum_mm, 1)
                    pe.wait_ge(wmean_ok, 1)
                values(g, 1)

            pe.wait_ge(consts, 11)
            transpose_x(0, 0)
            transpose_x(0, 1)
            pe.wait_ge(g_in, 32)
            nc.tensor.matmul(AV_BANK[:, 0:2], ones[0:1, :], gin[0:1, :], start=True, stop=True).then_inc(sum_mm, 1)
            qk(0, (0,))
            group(0, first=True)
            with pe.Fori(1, 3) as g:
                group(g)
            group(3, scales=True)
            with pe.Fori(4, 7) as g:
                group(g)
            group(7, last=True)

            def transpose_o(i, u):
                pe.wait_ge(ot_in[u], 16 * i + 16)
                pe.wait_ge(oT_lo_ok[u], i)
                for c in range(DC):
                    ins = nc.tensor.transpose(banks[u][:, c * P:(c + 1) * P], ot[:, u, c * P:(c + 1) * P], ident[:, :])
                ins.then_inc(ot_mm[u], 1)

            def project(i, u):
                pe.wait_ge(oT_lo_ok[u], i + 1)
                pe.wait_ge(wo_lo_ok, 1)
                pe.wait_ge(x1_ok[u], i)
                products(banks[2 + u][:, :], [(oT[a][:, u, c, :], wo[b][:, c, :])
                                              for c in range(DC) for a, b in PASSES]).then_inc(pr_mm[u], 1)

            def pair(i):
                transpose_o(i, 1)
                project(i, 0)
                transpose_o(i + 1, 0)
                project(i, 1)

            transpose_o(0, 0)
            pair(0)
            with pe.Fori(1, PAIRS - 1) as i:
                pair(i)
            transpose_o(PAIRS - 1, 1)
            project(PAIRS - 1, 0)
            project(PAIRS - 1, 1)

            def transpose_xq(i, u):
                pe.wait_ge(xq_ok[u], i + 1)
                pe.wait_ge(xqT_ok[1 - u], i + u)
                for c in range(DC):
                    ins = nc.tensor.transpose(XQ_PS[:, c, :], xq[:, u, c * P:(c + 1) * P], identb[:, :])
                ins.then_inc(xq_mm[u], 1)

            def up(i, u, j):
                a, n = HCH[j]
                k, turn = bank_turn(u, j)
                pe.wait_ge(xqT_ok[u], i + 1)
                pe.wait_ge(h_ok[k], 3 * i + turn)
                products(banks[k][:, 0:n], [(xqT[:, u, c, :], WQ[:, c, a:a + n]) for c in range(DC)])
                products(banks[2 + k][:, 0:n], [(xqT[:, u, c, :], WQ[:, 4 + c, a:a + n])
                                                for c in range(DC)]).then_inc(ab_mm[k], 1)

            def transpose_h(i, u):
                pe.wait_ge(hq_ok[u], 2 * i + 2)
                pe.wait_ge(hT_a[1 - u], i + u)
                pe.wait_ge(hT_b[1 - u], i + u)
                for c in range(FC):
                    ins = nc.tensor.transpose(H_PS[c // 8][:, c % 8, :], hq[:, u, c * P:(c + 1) * P], identb[:, :])
                ins.then_inc(h_mm[u], 1)

            def down(i, u):
                pe.wait_ge(hT_a[u], i + 1)
                pe.wait_ge(hT_b[u], i + 1)
                pe.wait_ge(y_ok[1 - u], i + u)
                products(banks[7][:, :], [(hqT[:, u, c, :], w2q[:, c, :]) for c in range(FC)]).then_inc(w2_mm[u], 1)

            def tile(i, u, first=False, last=False):
                up(i, u, 0)
                up(i, u, 1)
                if not first:
                    transpose_h(i + u - 1, 1 - u)
                up(i, u, 2)
                if not last:
                    transpose_xq(i + u, 1 - u)
                if not first:
                    down(i + u - 1, 1 - u)

            transpose_xq(0, 0)
            for s in x1_ok:
                pe.wait_ge(s, PAIRS)
            tile(0, 0, first=True)
            tile(0, 1)
            with pe.Fori(1, PAIRS - 1) as i:
                tile(i, 0)
                tile(i, 1)
            tile(PAIRS - 1, 0)
            tile(PAIRS - 1, 1, last=True)
            transpose_h(PAIRS - 1, 1)
            down(PAIRS - 1, 1)


def kernel(x, ctx_2048, mask_BxSx4224_bf0, g_xattn, g_ffn, L0_xattn_wq, L0_xattn_wk, L0_xattn_wv, L0_xattn_wo,
           L0_ffn_w1, L0_ffn_w2, L0_ffn_w3):
    import concourse.bacc as bacc
    from concourse.bass_utils import run_bass_kernel_spmd

    def chunks(w):
        w = np.asarray(w)
        return np.ascontiguousarray(w.T.reshape(w.shape[1] // P, P, w.shape[0]).transpose(1, 0, 2))

    c = np.asarray(ctx_2048)
    keys = c.reshape(B, CK, 3, DC, P).transpose(0, 4, 3, 2, 1).reshape(B, P, DC, KC)
    ffn = np.concatenate([chunks(L0_ffn_w1).transpose(1, 0, 2), chunks(L0_ffn_w3).transpose(1, 0, 2),
                          chunks(L0_ffn_w2).reshape(P, 4, F).transpose(1, 0, 2)])
    arrays = {
        "x": np.ascontiguousarray(np.asarray(x).reshape(TOK, D)),
        "ctxT": np.ascontiguousarray(keys),
        "ctx": np.ascontiguousarray(c.reshape(B, CK, 3, D)),
        "g_xattn": np.ascontiguousarray(g_xattn),
        "g_ffn": np.ascontiguousarray(g_ffn),
        "wqT": chunks(L0_xattn_wq), "wkT": chunks(L0_xattn_wk), "wvT": chunks(L0_xattn_wv), "woT": chunks(L0_xattn_wo),
        "wffn": np.ascontiguousarray(ffn),
    }
    nc = bacc.Bacc("TRN2", target_bir_lowering=False, num_devices=1)
    ins = [nc.dram_tensor(n, a.shape, mybir.dt.from_np(a.dtype), kind="ExternalInput").ap() for n, a in arrays.items()]
    out = nc.dram_tensor("out", (TOK, D), mybir.dt.float32, kind="ExternalOutput").ap()
    o_dram = nc.dram_tensor("o_dram", (TOK, D), mybir.dt.float32, kind="Internal").ap()
    flamingo_kernel(nc, *ins, out, o_dram)
    r = run_bass_kernel_spmd(nc, [arrays], core_ids=[0])
    return np.asarray(r.results[0]["out"]).reshape(B, TQ, D)
```

```python
from contextlib import ExitStack

import numpy as np

import concourse.bass as bass
from concourse import mybir

B, TQ, D = 16, 112, 512
KC = 375
F = 1408
P = 128
DC = D // P
FC = F // P
CK = KC // 3
KEYS = KC + TQ
KPAD = KEYS + 1
PPAD = 4 * CK
TOK = B * TQ
NT = TOK // P
GROUPS = B // 2
PAIRS = NT // 2
EPS = 1e-5
SCALE = float(D) ** -0.5
MAGIC = 12582912.0
WCH = 12
NW = float(F * D)
HCH = [(0, 512), (512, 512), (1024, 384)]


def flamingo_kernel(nc, x, ctxT, ctx, g_xattn, g_ffn, wqT, wkT, wvT, woT, wffn, out, o_dram):
    fp32 = mybir.dt.float32
    f32r = mybir.dt.float32r
    bf16 = mybir.dt.bfloat16
    ALU = mybir.AluOpType
    ACT = mybir.ActivationFunctionType
    AX = mybir.AxisListType.X

    x_b = x.rearrange("(n t) d -> n t d", t=TQ)
    o_b = o_dram.rearrange("(n t) d -> n t d", t=TQ)
    x_t = x.rearrange("(n p) d -> n p d", p=P)
    o_t = o_dram.rearrange("(n p) d -> n p d", p=P)
    y_t = out.rearrange("(n p) d -> n p d", p=P)

    keep = ExitStack()
    with keep:
        def sb(name, shape, dt, stack=keep):
            return stack.enter_context(nc.sbuf_tensor(name, shape, dt))

        def sem(name):
            return keep.enter_context(nc.semaphore(name))

        def sems(name, n=2):
            return [sem(f"{name}{i}") for i in range(n)]

        banks = [keep.enter_context(nc.psum_tensor(f"bank{i}", [P, 512], fp32)) for i in range(8)]

        WQ = sb("ffn_ternary", [P, WCH, F], bf16)
        w2q = WQ[:, 8:12, :].rearrange("p a f -> p (a f)").rearrange("p (c n) -> p c n", n=D)
        wbuf = sb("ffn_raw", [P, 2, F], fp32)
        ident = sb("ident", [P, P], fp32)
        identb = sb("identb", [P, P], bf16)
        ones = sb("ones", [P, P], fp32)
        magic = sb("magic", [P, 2], fp32)
        epsc = sb("epsc", [P, 1], fp32)
        gin = sb("gin", [1, 2], fp32)
        gates = sb("gates", [P, 2], fp32)
        wabs = sb("wabs", [P, WCH], fp32)
        wabs3 = sb("wabs3", [P, 3], fp32)
        wmean = sb("wmean", [P, 3], fp32)
        wscale = sb("wscale", [P, 3], fp32)
        wscur = sb("wscur", [P, 1], fp32)
        bn = sb("bn", [TQ, 2, 6], fp32)
        mv = sb("mv", [TQ, 2, 2], fp32)
        warm = sb("warm", [P, 1], fp32)
        std = sb("std", [TQ, 2], fp32)
        rstd = sb("rstd", [TQ, 2], fp32)
        rowmax = sb("rowmax", [TQ, 2], fp32)
        expbias = sb("expbias", [TQ, 2], fp32)
        rowsum = sb("rowsum", [TQ, 2], fp32)
        rowinv = sb("rowinv", [TQ, 2], fp32)

        half1 = ExitStack()
        wsp = [[sb(f"{w}_{s}", [P, DC, D], f32r, half1) for s in ("hi", "lo")] for w in ("wq", "wk", "wv")]
        kraw = sb("kraw", [P, DC, KC], fp32, half1)
        vraw = sb("vraw", [CK, 3, D], fp32, half1)
        vv = [sb(f"v_{s}", [P, 2, 4, D], f32r, half1) for s in ("hi", "lo")]
        kT = [sb(f"kT_{s}", [P, 2, DC, KPAD], f32r, half1) for s in ("hi", "lo")]
        xT = [sb(f"xT_{s}", [P, DC, 2 * TQ], f32r, half1) for s in ("hi", "lo")]
        qT = [sb(f"qT_{s}", [P, DC, 2 * TQ], f32r, half1) for s in ("hi", "lo")]
        xb = sb("xb", [TQ, 2, D], fp32, half1)
        prob = sb("prob", [TQ, 2, PPAD], fp32, half1)
        pT = [sb(f"pT_{s}", [CK, 2, 4 * TQ], f32r, half1) for s in ("hi", "lo")]
        ob = sb("ob", [TQ, 2, D], fp32, half1)
        half1.close()
        start = ExitStack()
        for w in ("wq", "wk", "wv"):
            for s in ("hi", "lo"):
                sb(f"skip_{w}_{s}", [P, DC, D], f32r, start)
        sb("skip_kraw", [P, DC, KC], fp32, start)
        sb("skip_vraw", [CK, 3, D], fp32, start)
        wraw = sb("wraw", [P, 3, DC, D], fp32, start)
        start.close()

        half2 = ExitStack()
        wo = [sb(f"wo_{s}", [P, DC, D], f32r, half2) for s in ("hi", "lo")]
        x1 = sb("x1", [P, NT, D], fp32, half2)
        ot = sb("ot", [P, 2, D], fp32, half2)
        oT = [sb(f"oT_{s}", [P, 2, DC, P], f32r, half2) for s in ("hi", "lo")]
        bn2 = sb("bn2", [P, NT * 6], fp32, half2)
        mv2 = sb("mv2", [P, NT, 2], fp32, half2)
        std2 = sb("std2", [P, NT], fp32, half2)
        rstd2 = sb("rstd2", [P, NT], fp32, half2)
        nmean2 = sb("nmean2", [P, NT], fp32, half2)
        wdq = sb("wdq", [P, 3], fp32, half2)
        xc = sb("xc", [P, 2, D], fp32, half2)
        xq = sb("xq", [P, 2, D], bf16, half2)
        xqT = sb("xqT", [P, 2, DC, P], bf16, half2)
        hid = sb("hid", [P, 2, F], fp32, half2)
        hq = sb("hq", [P, 2, F], bf16, half2)
        hqT = sb("hqT", [P, 2, FC, P], bf16, half2)
        yb = sb("yb", [P, 2, D], fp32, half2)
        col = {n: sb(n, [P, 2], fp32, half2) for n in ("xamax", "xclip", "xinv", "xmul", "hclip", "hinv", "hmul", "ydq")}
        hamax = sb("hamax", [P, 2, 2], fp32, half2)
        xdq = sb("xdq", [P, 2, 2], fp32, half2)
        half2.close()

        consts = sem("consts")
        g_in, sum_mm, gates_ok = sem("g_in"), sem("sum_mm"), sem("gates_ok")
        pw_in, pw_hi, pw_lo = sems("pw_in", 4), sem("pw_hi"), sem("pw_lo")
        x_in, bn_ok, mv_ok = sems("x_in"), sems("bn_ok"), sem("mv_ok")
        std_ok, rstd_ok, xn_ok = sem("std_ok"), sem("rstd_ok"), sems("xn_ok")
        t_mm, xT_hi, xT_lo = sems("t_mm"), sems("xT_hi_ok"), sems("xT_lo_ok")
        qk_mm, qk_hi, qk_lo = sems("qk_mm"), sems("qk_hi"), sems("qk_lo")
        v_mm, v_hi, v_lo = sems("v_mm"), sems("v_hi_ok"), sems("v_lo_ok")
        k_in, k_hi, k_split = sems("k_in"), sems("k_hi"), sems("k_split")
        v_in, vc_hi, v_split = sems("v_in"), sems("vc_hi"), sems("v_split")
        s_mm, max_ok, bias_ok, exp_ok = sems("s_mm"), sems("max_ok"), sems("bias_ok"), sems("exp_ok")
        inv_ok, pt_mm, pt_hi, pt_lo = sems("inv_ok"), sems("pt_mm"), sems("pt_hi"), sems("pt_lo")
        av_mm, o_ok, o_out = sems("av_mm"), sems("o_ok"), sems("o_out")
        w_in, w_used = sems("w_in"), sems("w_used")
        wabs_ok, wmean_ok, wscale_ok = sem("wabs_ok"), sem("wmean_ok"), sem("wscale_ok")
        wscur_ok, wround_ok = sem("wscur_ok"), sem("wround_ok")
        wo_in, wo_hi_ok, wo_lo_ok = sem("wo_in"), sem("wo_hi_ok"), sem("wo_lo_ok")
        pool_go, dve_go = sem("pool_go"), sem("dve_go")
        ot_in, x1_in = sems("ot_in"), sem("x1_in")
        ot_mm, oT_hi_ok, oT_lo_ok = sems("ot_mm"), sems("oT_hi_ok"), sems("oT_lo_ok")
        pr_mm, x1_ok, bn2_ok = sems("pr_mm"), sems("x1_ok"), sem("bn2_ok")
        mv2_ok, nmean2_ok, std2_ok, rstd2_ok, wdq_ok = (sem(n) for n in ("mv2_ok", "nmean2_ok", "std2_ok", "rstd2_ok", "wdq_ok"))
        xc_ok, xamax_ok, xinv_ok = sems("xc_ok"), sems("xamax_ok"), sems("xinv_ok")
        xmul_ok, xdq_ok, xr_ok, xq_ok = sems("xmul_ok"), sems("xdq_ok"), sems("xr_ok"), sems("xq_ok")
        xq_mm, xqT_ok = sems("xq_mm"), sems("xqT_ok")
        ab_mm, h_ok, silu_ok = sems("ab_mm"), sems("h_ok"), sems("silu_ok")
        hamax_ok, hclip_ok, hinv_ok, hmul_ok, ydq_ok = (sems(n) for n in ("hamax_ok", "hclip_ok", "hinv_ok", "hmul_ok", "ydq_ok"))
        last_r = sem("last_r")
        hr_ok, hq_ok, h_mm, hT_a, hT_b = sems("hr_ok"), sems("hq_ok"), sems("h_mm"), sems("hT_a"), sems("hT_b")
        w2_mm, y_ok, y_out = sems("w2_mm"), sems("y_ok"), sems("y_out")

        HALVES = (slice(0, 6 * P), slice(6 * P, F))
        HI, LO = 0, 1
        PW = [(0, slice(0, D // 2)), (0, slice(D // 2, D)), (1, slice(0, D)), (2, slice(0, D))]
        PASSES = [(HI, HI), (HI, LO), (LO, HI)]
        Q_BANK, R_BANK, S_BANK = banks[0:2], banks[2:4], banks[4:6]
        PT_BANK, AV_BANK = banks[6], banks[7]

        SPARE = banks[5], banks[6]
        XQ_PS = banks[4][:, 0:2 * P].bitcast(bf16).rearrange("p (c t) -> p c t", c=DC)
        H_PS = [banks[5][:, 0:4 * P].bitcast(bf16).rearrange("p (c t) -> p c t", c=8),
                banks[6][:, 0:3 * P // 2].bitcast(bf16).rearrange("p (c t) -> p c t", c=3)]

        def k_new(bank):
            return bank[:, 0:4 * TQ].rearrange("p (e u t) -> p u e t", e=2, u=2)

        def two(bank):
            return bank[:, 0:4 * TQ].rearrange("p (e t) -> p e t", e=2)

        def four(bank, n):
            return bank[:, 0:4 * n].rearrange("p (c t) -> p c t", c=4)

        def fr(ap):
            return ap.bitcast(fp32)

        def first_half_over(eng):
            for u in range(2):
                eng.wait_ge(o_ok[u], GROUPS)
                eng.wait_ge(o_out[u], 16 * GROUPS)

        def bank_turn(u, j):
            return (3 * u + j) % 2, (3 * u + j) // 2

        block = keep.enter_context(nc.Block())

        @block.sync
        def _(eng):
            def load_x(g, u):
                eng.wait_ge(t_mm[u], g)
                eng.dma_start(xb[:, u, :], x_b[bass.ds(2 * g + u, 1), :, :].rearrange("a t d -> (a t) d")).then_inc(x_in[u], 16)

            def load_k(g, u):
                if not (isinstance(g, int) and g == 0 and u == 0):
                    eng.wait_ge(k_split[1 - u], g + u)
                eng.dma_start(kraw[:, :, :], ctxT[bass.ds(2 * g + u, 1), :, :, :].rearrange("a p c k -> (a p) c k")).then_inc(k_in[u], 16)

            def load_v(g, u):
                if not (isinstance(g, int) and g == 0 and u == 0):
                    eng.wait_ge(v_split[1 - u], g + u)
                eng.dma_start(vraw[:, :, :], ctx[bass.ds(2 * g + u, 1), :, :, :].rearrange("a p c d -> (a p) c d")).then_inc(v_in[u], 16)

            def load_w(chunk, turn, j):
                eng.wait_ge(w_used[j % 2], turn + j // 2)
                eng.dma_start(wbuf[:, j % 2, :], wffn[bass.ds(chunk + j, 1), :, :].rearrange("a p f -> (a p) f")).then_inc(w_in[j % 2], 16)

            def store_o(g, u):
                eng.wait_ge(o_ok[u], g + 1)
                eng.dma_start(o_b[bass.ds(2 * g + u, 1), :, :].rearrange("a t d -> (a t) d"), ob[:, u, :]).then_inc(o_out[u], 16)

            def group(g, w=None, more=True, first=False):
                if w:
                    load_w(*w, 0)
                load_v(g, 1)
                if not first:
                    store_o(g - 1, 0)
                    store_o(g - 1, 1)
                if w:
                    load_w(*w, 1)
                load_k(g + 1, 0)
                if w:
                    load_w(*w, 2)
                load_v(g + 1, 0)
                if w:
                    load_w(*w, 3)
                load_k(g + 1, 1)
                if more:
                    load_x(g + 2, 0)
                    load_x(g + 2, 1)

            for u in range(2):
                eng.dma_start(xb[:, u, :], x_b[u, :, :]).then_inc(x_in[u], 16)
            for n, e in enumerate((slice(0, D // 2), slice(D // 2, D))):
                eng.dma_start(wraw[:, 0, :, e], wqT[:, :, e]).then_inc(pw_in[n], 16)
            eng.dma_start(gin[0:1, 0:1], g_xattn.rearrange("(a b) -> a b", a=1)).then_inc(g_in, 16)
            eng.dma_start(gin[0:1, 1:2], g_ffn.rearrange("(a b) -> a b", a=1)).then_inc(g_in, 16)
            eng.dma_start(wraw[:, 1, :, :], wkT).then_inc(pw_in[2], 16)
            load_k(0, 0)
            eng.dma_start(wraw[:, 2, :, :], wvT).then_inc(pw_in[3], 16)
            load_v(0, 0)
            load_x(1, 0)
            load_x(1, 1)
            load_k(0, 1)
            group(0, (0, 0), first=True)
            with eng.Fori(1, 3) as g:
                group(g, (4 * g, 2 * g))
            group(3)
            with eng.Fori(4, 6) as g:
                group(g, (4 * g - 16, 2 * g - 2))
            group(6, (8, 10), more=False)
            load_v(7, 1)
            store_o(6, 0)
            store_o(6, 1)
            for s in w_used:
                eng.wait_ge(s, 12)
            eng.dma_start(wbuf[:, :, :].rearrange("p a f -> p (a f)")[:, 0:DC * D].rearrange("p (c n) -> p c n", c=DC), woT).then_inc(wo_in, 16)
            for u in range(2):
                eng.wait_ge(qk_mm[u], 2 * GROUPS)
                eng.wait_ge(v_mm[u], GROUPS)
            def load_o(i, u):
                eng.wait_ge(ot_mm[u], i)
                eng.dma_start(ot[:, u, :], o_t[bass.ds(2 * i + u, 1), :, :].rearrange("a p d -> (a p) d")).then_inc(ot_in[u], 16)

            def load_x1(i, first=False):
                if not first:
                    eng.wait_ge(x1_in, 16 * i)
                eng.dma_start(x1[:, bass.ds(2 * i, 2), :], x_t[bass.ds(2 * i, 2), :, :].rearrange("n p d -> p n d")).then_inc(x1_in, 16)

            for u in range(2):
                eng.wait_ge(o_out[u], 16 * (GROUPS - 1))
                load_o(0, u)
            load_x1(0, first=True)
            load_o(1, 0)
            load_o(1, 1)
            load_x1(1)
            store_o(7, 0)
            store_o(7, 1)
            with eng.Fori(2, PAIRS - 1) as i:
                load_o(i, 0)
                load_o(i, 1)
                load_x1(i)
            load_x1(PAIRS - 1)
            for u in range(2):
                eng.wait_ge(o_out[u], 16 * GROUPS)
                load_o(PAIRS - 1, u)
            with eng.Fori(0, PAIRS) as i:
                for u in range(2):
                    eng.wait_ge(y_ok[u], i + 1)
                    eng.dma_start(y_t[bass.ds(2 * i + u, 1), :, :].rearrange("a p d -> (a p) d"), yb[:, u, :]).then_inc(y_out[u], 16)
            for u in range(2):
                eng.wait_ge(y_out[u], 16 * PAIRS)

        @block.gpsimd
        def _(eng):
            eng.memset(ident[:, :], 0.0).then_inc(consts, 1)
            eng.memset(identb[:, :], 0.0).then_inc(consts, 1)
            eng.memset(ones[:, :], 1.0).then_inc(consts, 1)
            eng.memset(magic[:, 0:1], MAGIC).then_inc(consts, 1)
            eng.memset(magic[:, 1:2], -MAGIC).then_inc(consts, 1)
            eng.memset(epsc[:, :], EPS).then_inc(consts, 1)
            for half in kT:
                eng.memset(half[:, :, :, KEYS:KPAD].bitcast(fp32), 0.0).then_inc(consts, 1)
            eng.memset(prob[:, :, KEYS:PPAD], 0.0).then_inc(consts, 1)
            eng.wait_ge(consts, 9)
            for m in (ident, identb):
                eng.affine_select(out=m[:, :], in_=m[:, :], compare_op=ALU.not_equal, fill=1.0,
                                  base=0, pattern=[[-1, P]], channel_multiplier=1).then_inc(consts, 1)
            def split(g, u):
                eng.wait_ge(k_in[u], 16 * g + 16)
                eng.wait_ge(s_mm[u], g)
                eng.sem_inc(pool_go, 1)
                eng.tensor_scalar(kT[HI][:, u, :, 0:KC], kraw[:, :, :], 1.0, 0.0, ALU.mult, ALU.add).then_inc(k_hi[u], 1)
                eng.wait_ge(k_hi[u], g + 1)
                eng.tensor_tensor(kT[LO][:, u, :, 0:KC], kraw[:, :, :], fr(kT[HI][:, u, :, 0:KC]), ALU.subtract).then_inc(k_split[u], 1)
                eng.wait_ge(pw_lo, len(PW))
                eng.wait_ge(v_in[u], 16 * g + 16)
                eng.wait_ge(av_mm[u], g)
                eng.sem_inc(pool_go, 1)
                eng.tensor_scalar(vv[HI][0:CK, u, 0:3, :], vraw[:, :, :], 1.0, 0.0, ALU.mult, ALU.add).then_inc(vc_hi[u], 1)
                eng.wait_ge(vc_hi[u], g + 1)
                eng.tensor_tensor(vv[LO][0:CK, u, 0:3, :], vraw[:, :, :], fr(vv[HI][0:CK, u, 0:3, :]), ALU.subtract).then_inc(v_split[u], 1)

            for u in range(2):
                split(0, u)
            with eng.Fori(1, GROUPS) as g:
                for u in range(2):
                    split(g, u)

            def quant_x(i, u):
                eng.wait_ge(xmul_ok[u], i + 1)
                eng.sem_inc(pool_go, 1)
                eng.tensor_scalar(xc[:, u, :], xc[:, u, :], col["xmul"][:, u:u + 1], MAGIC, ALU.mult, ALU.add).then_inc(xr_ok[u], 1)
                eng.wait_ge(xr_ok[u], i + 1)
                eng.wait_ge(xq_mm[u], i)
                eng.sem_inc(pool_go, 1)
                eng.tensor_scalar(xq[:, u, :], xc[:, u, :], -MAGIC, 1.0, ALU.add, ALU.mult).then_inc(xq_ok[u], 1)

            def quant_h(i, u, halves=HALVES):
                for n, a in enumerate(halves):
                    eng.wait_ge(hr_ok[u], 2 * i + n + 1)
                    eng.wait_ge(h_mm[u], i)
                    eng.sem_inc(pool_go, 1)
                    eng.tensor_scalar(hq[:, u, a], hid[:, u, a], -MAGIC, 1.0, ALU.add, ALU.mult).then_inc(hq_ok[u], 1)

            for u in range(2):
                quant_x(0, u)
            for u in range(2):
                quant_h(0, u)
                quant_x(1, u)
            with eng.Fori(1, PAIRS - 1) as i:
                for u in range(2):
                    quant_h(i, u)
                    quant_x(i + 1, u)
            quant_h(PAIRS - 1, 0)
            quant_h(PAIRS - 1, 1, HALVES[0:1])

        @block.scalar
        def _(act):
            def std_of(g):
                act.wait_ge(mv_ok, 2 * g + 2)
                nc.scalar.activation(std[:, :], mv[:, :, 1], ACT.Sqrt, bias=epsc[0:TQ, 0:1]).then_inc(std_ok, 1)

            def x_hi(g, u):
                act.wait_ge(t_mm[u], g + 1)
                act.wait_ge(v_mm[0], g)
                act.wait_ge(v_mm[1], g)
                nc.scalar.copy(xT[HI][:, :, u * TQ:(u + 1) * TQ], four(R_BANK[u], TQ)).then_inc(xT_hi[u], 1)

            def qk(g, j):
                act.wait_ge(qk_mm[j % 2], 2 * g + j // 2 + 1)
                if j == 0:
                    for u in range(2):
                        act.wait_ge(s_mm[u], g)
                if j < 2:
                    nc.scalar.copy(qT[HI][:, 2 * j:2 * j + 2, :], two(Q_BANK[j % 2])).then_inc(qk_hi[j % 2], 1)
                else:
                    e = 2 * (j - 2)
                    nc.scalar.copy(kT[HI][:, :, e:e + 2, KC:KEYS], k_new(Q_BANK[j % 2])).then_inc(qk_hi[j % 2], 1)

            def v(g, u):
                act.wait_ge(v_mm[u], g + 1)
                act.wait_ge(av_mm[u], g)
                act.wait_ge(pw_lo, len(PW))
                nc.scalar.copy(vv[HI][0:TQ, u, 3, :], R_BANK[u][0:TQ, :]).then_inc(v_hi[u], 1)

            def exp(g, u):
                act.wait_ge(bias_ok[u], g + 1)
                act.wait_ge(pt_mm[u], g)
                nc.scalar.activation(prob[:, u, 0:KEYS], S_BANK[u][0:TQ, 0:KEYS], ACT.Exp, bias=expbias[:, u:u + 1],
                                     scale=SCALE, accum_out=rowsum[:, u:u + 1]).then_inc(exp_ok[u], 1)

            def pt(g, u):
                act.wait_ge(pt_mm[u], g + 1)
                act.wait_ge(av_mm[u], g)
                nc.scalar.copy(pT[HI][:, u, :], PT_BANK[0:CK, 0:4 * TQ]).then_inc(pt_hi[u], 1)

            def o(g, u):
                act.wait_ge(av_mm[u], g + 1)
                act.wait_ge(inv_ok[u], g + 1)
                act.wait_ge(o_out[u], 16 * g)
                nc.scalar.activation(ob[:, u, :], AV_BANK[0:TQ, :], ACT.Copy, scale=rowinv[:, u:u + 1]).then_inc(o_ok[u], 1)

            def oT_high(i, u):
                act.wait_ge(ot_mm[u], i + 1)
                act.wait_ge(pr_mm[u], i)
                nc.scalar.copy(oT[HI][:, u, :, :], four(banks[u], P)).then_inc(oT_hi_ok[u], 1)

            def round_w(g, j):
                s = j % 2
                act.wait_ge(w_in[s], 16 * (2 * g - 2 + j // 2) + 16)
                nc.scalar.activation(wbuf[:, s, :], wbuf[:, s, :], ACT.Identity, bias=magic[:, 0:1],
                                     scale=wscur[:, 0:1]).then_inc(wround_ok, 1)

            def sign_w(g, j):
                s = j % 2
                act.wait_ge(wround_ok, 4 * g - 16 + j + 1)
                nc.scalar.activation(WQ[:, bass.ds(4 * g - 16 + j, 1), :].rearrange("p a f -> p (a f)"), wbuf[:, s, :],
                                     ACT.Sign, bias=magic[:, 1:2]).then_inc(w_used[s], 1)

            def group(g, w=False, first=False, last=False):
                if w:
                    act.wait_ge(wscale_ok, 1)
                    act.wait_ge(w_used[1], 2 * g - 2)
                    nc.scalar.copy(wscur[:, 0:1], wscale[:, bass.ds(g - 4, 1)]).then_inc(wscur_ok, 1)
                    act.wait_ge(wscur_ok, g - 3)
                    round_w(g, 0)
                qk(g, 1)
                if w:
                    sign_w(g, 0)
                qk(g, 2)
                if w:
                    round_w(g, 1)
                qk(g, 3)
                if last:
                    act.wait_ge(wo_in, 16)
                    for s in qk_mm:
                        act.wait_ge(s, 2 * GROUPS - 1)
                    nc.scalar.copy(wo[HI][:, :, :], raw_wo).then_inc(wo_hi_ok, 1)
                else:
                    std_of(g + 1)
                v(g, 0)
                if first:
                    act.wait_ge(sum_mm, 1)
                    nc.scalar.activation(gates[:, :], AV_BANK[:, 0:2], ACT.Tanh).then_inc(gates_ok, 1)
                exp(g, 0)
                if w:
                    sign_w(g, 1)
                v(g, 1)
                pt(g, 0)
                if w:
                    round_w(g, 2)
                if not last:
                    x_hi(g + 1, 0)
                    x_hi(g + 1, 1)
                exp(g, 1)
                if last:
                    for u in range(2):
                        act.wait_ge(k_split[u], GROUPS)
                        act.wait_ge(v_split[u], GROUPS)
                    oT_high(0, 0)
                o(g, 0)
                pt(g, 1)
                if w:
                    sign_w(g, 2)
                    round_w(g, 3)
                    sign_w(g, 3)
                if last:
                    oT_high(0, 1)
                else:
                    qk(g + 1, 0)
                o(g, 1)

            raw_wo = wbuf[:, :, :].rearrange("p a f -> p (a f)")[:, 0:DC * D].rearrange("p (c n) -> p c n", c=DC)
            act.wait_ge(consts, 11)
            nc.scalar.activation(warm[:, :], epsc[:, :], ACT.Sqrt)
            std_of(0)
            for n, (i, e) in enumerate(PW):
                if n == 3:
                    qk(0, 0)
                act.wait_ge(pw_in[n], 16)
                nc.scalar.copy(wsp[i][HI][:, :, e], wraw[:, i, :, e]).then_inc(pw_hi, 1)
                if n == 0:
                    x_hi(0, 0)
                    x_hi(0, 1)
            group(0, first=True)
            with act.Fori(1, 3) as g:
                group(g)
            group(3)
            with act.Fori(4, 7) as g:
                group(g, w=True)
            group(7, last=True)

            def deviations(first, last):
                act.wait_ge(mv2_ok, last)
                nc.scalar.activation(std2[:, first:last], mv2[:, first:last, 1], ACT.Sqrt, bias=epsc[:, 0:1]).then_inc(std2_ok, 1)

            def center(i, u):
                act.wait_ge(xq_ok[u], i)
                nc.scalar.activation(xc[:, u, :], x1[:, bass.ds(2 * i + u, 1), :].rearrange("p a d -> p (a d)"),
                                     ACT.Identity, bias=nmean2[:, bass.ds(2 * i + u, 1)]).then_inc(xc_ok[u], 1)

            def silu(i, u, j, first=False):
                c, n = HCH[j]
                k, turn = bank_turn(u, j)
                a = SPARE[0] if first and j == 2 else banks[k]
                act.wait_ge(ab_mm[k], 3 * i + turn + 1)
                if j == 0:
                    act.wait_ge(xdq_ok[u], i + 1)
                    act.wait_ge(hq_ok[u], 2 * i)
                nc.scalar.activation(hid[:, u, c:c + n], a[:, 0:n], ACT.Silu,
                                     scale=xdq[:, u, 0:1]).then_inc(silu_ok[u], 1)

            def xqT_copy(i, u):
                act.wait_ge(xq_mm[u], i + 1)
                nc.scalar.copy(xqT[:, u, :, :], XQ_PS).then_inc(xqT_ok[u], 1)

            def hT_copy(i, u, n=8):
                act.wait_ge(h_mm[u], i + 1)
                act.wait_ge(w2_mm[u], i)
                nc.scalar.copy(hqT[:, u, 0:n, :], H_PS[0][:, 0:n, :]).then_inc(hT_a[u], 1)

            def round_h(i, u, halves=HALVES):
                act.wait_ge(hmul_ok[u], i + 1)
                for a in halves:
                    nc.scalar.activation(hid[:, u, a], hid[:, u, a], ACT.Identity, bias=magic[:, 0:1],
                                         scale=col["hmul"][:, u:u + 1]).then_inc(hr_ok[u], 1)

            def tile(i, u):
                silu(i, u, 0)
                silu(i, u, 1)
                hT_copy(i + u - 1, 1 - u)
                silu(i, u, 2)
                xqT_copy(i + u, 1 - u)
                center(i + 1, u)
                round_h(i, u)

            def end_pair(i, first=False, last=False):
                silu(i, 0, 0)
                silu(i, 0, 1)
                if not first:
                    hT_copy(i - 1, 1)
                    xqT_copy(i, 1)
                silu(i, 0, 2, first)
                if not last:
                    center(i + 1, 0)
                silu(i, 1, 0)
                round_h(i, 0)
                silu(i, 1, 1)
                silu(i, 1, 2)
                hT_copy(i, 0)
                if not last:
                    xqT_copy(i + 1, 0)
                    center(i + 1, 1)
                round_h(i, 1, HALVES[0:1] if last else HALVES)

            oT_high(1, 0)
            first_half_over(act)
            oT_high(1, 1)
            deviations(0, 2)
            with act.Fori(2, 4) as i:
                oT_high(i, 0)
                oT_high(i, 1)
            act.wait_ge(nmean2_ok, 1)
            center(0, 0)
            center(0, 1)
            with act.Fori(4, PAIRS) as i:
                oT_high(i, 0)
                oT_high(i, 1)
            xqT_copy(0, 0)
            xqT_copy(0, 1)
            deviations(2, NT)
            act.wait_ge(nmean2_ok, 3)
            end_pair(0, first=True)
            with act.Fori(1, PAIRS - 1) as i:
                tile(i, 0)
                tile(i, 1)
            end_pair(PAIRS - 1, last=True)
            hT_copy(PAIRS - 1, 1, n=4)

        @block.vector
        def _(dve):
            V = nc.vector

            def stats(g):
                for u in range(2):
                    dve.wait_ge(x_in[u], 16 * g + 16)
                    V.bn_stats(bn[:, u, :], xb[:, u, :]).then_inc(bn_ok[u], 1)
                for u in range(2):
                    dve.wait_ge(bn_ok[u], g + 1)
                    dve.sem_inc(dve_go, 1)
                    V.bn_aggr(mv[:, u, :], bn[:, u, :]).then_inc(mv_ok, 1)

            def normalise(g):
                dve.wait_ge(std_ok, g + 1)
                V.reciprocal(rstd[:, :], std[:, :]).then_inc(rstd_ok, 1)
                dve.wait_ge(rstd_ok, g + 1)
                for u in range(2):
                    V.tensor_scalar(xb[:, u, :], xb[:, u, :], mv[:, u, 0:1], rstd[:, u:u + 1],
                                    ALU.subtract, ALU.mult).then_inc(xn_ok[u], 1)

            def x_lo(g, u):
                dve.wait_ge(xT_hi[u], g + 1)
                d = slice(u * TQ, (u + 1) * TQ)
                V.tensor_tensor(xT[LO][:, :, d], four(R_BANK[u], TQ), fr(xT[HI][:, :, d]), ALU.subtract).then_inc(xT_lo[u], 1)

            def qk(g, j):
                dve.wait_ge(qk_hi[j % 2], 2 * g + j // 2 + 1)
                if j < 2:
                    d = slice(2 * j, 2 * j + 2)
                    V.tensor_tensor(qT[LO][:, d, :], two(Q_BANK[j % 2]), fr(qT[HI][:, d, :]), ALU.subtract).then_inc(qk_lo[j % 2], 1)
                else:
                    e = 2 * (j - 2)
                    V.tensor_tensor(kT[LO][:, :, e:e + 2, KC:KEYS], k_new(Q_BANK[j % 2]),
                                    fr(kT[HI][:, :, e:e + 2, KC:KEYS]), ALU.subtract).then_inc(qk_lo[j % 2], 1)

            def v(g, u):
                dve.wait_ge(v_hi[u], g + 1)
                V.tensor_tensor(vv[LO][0:TQ, u, 3, :], R_BANK[u][0:TQ, :], fr(vv[HI][0:TQ, u, 3, :]),
                                ALU.subtract).then_inc(v_lo[u], 1)

            def rowmaxima(g, u):
                dve.wait_ge(s_mm[u], g + 1)
                V.tensor_reduce(rowmax[:, u:u + 1], S_BANK[u][0:TQ, 0:KEYS], AX, ALU.max).then_inc(max_ok[u], 1)
                dve.wait_ge(max_ok[u], g + 1)
                dve.wait_ge(exp_ok[u], g)
                V.tensor_scalar(expbias[:, u:u + 1], rowmax[:, u:u + 1], -SCALE, None, ALU.mult).then_inc(bias_ok[u], 1)

            def pt(g, u):
                dve.wait_ge(pt_hi[u], g + 1)
                V.tensor_tensor(pT[LO][:, u, :], PT_BANK[0:CK, 0:4 * TQ], fr(pT[HI][:, u, :]), ALU.subtract).then_inc(pt_lo[u], 1)
                dve.wait_ge(exp_ok[u], g + 1)
                dve.wait_ge(o_ok[u], g)
                V.reciprocal(rowinv[:, u:u + 1], rowsum[:, u:u + 1]).then_inc(inv_ok[u], 1)

            def magnitudes(g, j):
                dve.wait_ge(w_in[j % 2], 16 * (2 * g + j // 2) + 16)
                V.tensor_reduce(wabs[:, bass.ds(4 * g + j, 1)], wbuf[:, j % 2, :], AX, ALU.add,
                                apply_absolute_value=True).then_inc(w_used[j % 2], 1)

            def oT_low(i, u):
                dve.wait_ge(oT_hi_ok[u], i + 1)
                V.tensor_tensor(oT[LO][:, u, :, :], four(banks[u], P), fr(oT[HI][:, u, :, :]), ALU.subtract).then_inc(oT_lo_ok[u], 1)

            def group(g, w=False, scales=False, first=False, last=False):
                if not first:
                    qk(g, 1)
                    if w:
                        magnitudes(g, 0)
                qk(g, 2)
                if not last:
                    stats(g + 1)
                qk(g, 3)
                if w and not first:
                    magnitudes(g, 1)
                if scales:
                    for s in w_used:
                        dve.wait_ge(s, 6)
                    V.tensor_reduce(wabs3[:, :], wabs[:, :].rearrange("p (m c) -> p m c", c=4), AX, ALU.add).then_inc(wabs_ok, 1)
                v(g, 0)
                rowmaxima(g, 0)
                if last:
                    dve.wait_ge(wo_hi_ok, 1)
                    V.tensor_tensor(wo[LO][:, :, :], raw_wo, fr(wo[HI][:, :, :]), ALU.subtract).then_inc(wo_lo_ok, 1)
                if w:
                    magnitudes(g, 0 if first else 2)
                v(g, 1)
                if not last:
                    normalise(g + 1)
                pt(g, 0)
                rowmaxima(g, 1)
                if last:
                    for u in range(2):
                        dve.wait_ge(k_split[u], GROUPS)
                        dve.wait_ge(v_split[u], GROUPS)
                    oT_low(0, 0)
                else:
                    x_lo(g + 1, 0)
                    x_lo(g + 1, 1)
                if w:
                    magnitudes(g, 1 if first else 3)
                pt(g, 1)
                if scales:
                    dve.wait_ge(sum_mm, 2)
                    V.tensor_scalar(wmean[:, :], AV_BANK[:, 0:3], 1.0 / NW, EPS, ALU.mult, ALU.max).then_inc(wmean_ok, 1)
                    dve.wait_ge(wmean_ok, 1)
                    V.reciprocal(wscale[:, :], wmean[:, :]).then_inc(wscale_ok, 1)
                if not last:
                    qk(g + 1, 0)
                if first:
                    magnitudes(g, 2)
                    magnitudes(g, 3)

            raw_wo = wbuf[:, :, :].rearrange("p a f -> p (a f)")[:, 0:DC * D].rearrange("p (c n) -> p c n", c=DC)
            stats(0)
            normalise(0)
            for n, (i, e) in enumerate(PW):
                if n == 3:
                    qk(0, 0)
                    qk(0, 1)
                dve.wait_ge(pw_hi, n + 1)
                V.tensor_tensor(wsp[i][LO][:, :, e], wraw[:, i, :, e], fr(wsp[i][HI][:, :, e]), ALU.subtract).then_inc(pw_lo, 1)
                if n == 0:
                    x_lo(0, 0)
                    x_lo(0, 1)
            group(0, w=True, first=True)
            with dve.Fori(1, 3) as g:
                group(g, w=True)
            group(3, scales=True)
            with dve.Fori(4, 7) as g:
                group(g)
            group(7, last=True)

            dve.wait_ge(gates_ok, 1)

            def add(i, u):
                dve.wait_ge(pr_mm[u], i + 1)
                dve.wait_ge(x1_in, 16 * i + 16)
                t = x1[:, bass.ds(2 * i + u, 1), :].rearrange("p a d -> p (a d)")
                V.scalar_tensor_tensor(out=t, in0=banks[2 + u][:, :], scalar=gates[:, 0:1], in1=t,
                                       op0=ALU.mult, op1=ALU.add).then_inc(x1_ok[u], 1)
                dve.wait_ge(x1_ok[u], i + 1)
                V.bn_stats(bn2[:, bass.ds(12 * i + 6 * u, 6)], t).then_inc(bn2_ok, 1)

            def moments(first, last):
                dve.wait_ge(bn2_ok, last)
                for t in range(first, last):
                    V.bn_aggr(mv2[:, t, :], bn2[:, 6 * t:6 * t + 6]).then_inc(mv2_ok, 1)
                dve.wait_ge(mv2_ok, last)
                V.tensor_scalar(nmean2[:, first:last], mv2[:, first:last, 0], -1.0, None, ALU.mult).then_inc(nmean2_ok, 1)

            def deviations(first, last, n):
                dve.wait_ge(std2_ok, n)
                V.reciprocal(rstd2[:, first:last], std2[:, first:last]).then_inc(rstd2_ok, 1)
                dve.wait_ge(rstd2_ok, n)

            def pair(i):
                oT_low(i, 1)
                add(i, 0)
                oT_low(i + 1, 0)
                add(i, 1)

            c = {n: (lambda a: (lambda u: a[:, u:u + 1]))(a) for n, a in col.items()}

            def x_scale(i, u):
                r = rstd2[:, bass.ds(2 * i + u, 1)]
                dve.wait_ge(xc_ok[u], i + 1)
                V.tensor_reduce(c["xamax"](u), xc[:, u, :], AX, ALU.max, apply_absolute_value=True).then_inc(xamax_ok[u], 1)
                dve.wait_ge(xamax_ok[u], i + 1)
                V.tensor_scalar(c["xclip"](u), c["xamax"](u), r, EPS, ALU.mult, ALU.max).then_inc(xinv_ok[u], 1)
                dve.wait_ge(xinv_ok[u], 2 * i + 1)
                V.reciprocal(c["xinv"](u), c["xclip"](u)).then_inc(xinv_ok[u], 1)
                V.tensor_scalar(xdq[:, u, :], wdq[:, 0:2], c["xclip"](u), None, ALU.mult).then_inc(xdq_ok[u], 1)
                dve.wait_ge(xinv_ok[u], 2 * i + 2)
                V.tensor_scalar(c["xmul"](u), c["xinv"](u), 127.0, r, ALU.mult, ALU.mult).then_inc(xmul_ok[u], 1)

            def hidden(i, u, js, first=False):
                for j in js:
                    a, n = HCH[j]
                    k, turn = bank_turn(u, j)
                    b = SPARE[1] if first and j == 2 else banks[2 + k]
                    dve.wait_ge(silu_ok[u], 3 * i + j + 1)
                    dve.wait_ge(xdq_ok[u], i + 1)
                    V.scalar_tensor_tensor(out=hid[:, u, a:a + n], in0=b[:, 0:n], scalar=xdq[:, u, 1:2],
                                           in1=hid[:, u, a:a + n], op0=ALU.mult, op1=ALU.mult).then_inc(h_ok[k], 1)

            def h_max(i, u, part):
                need = ((1, 1), (2, 1))[part] if u == 0 else ((3, 2), (3, 3))[part]
                for k in range(2):
                    dve.wait_ge(h_ok[k], 3 * i + need[k])
                a = slice(0, 1024) if part == 0 else slice(1024, F)
                V.tensor_reduce(hamax[:, u, part:part + 1], hid[:, u, a], AX, ALU.max, apply_absolute_value=True).then_inc(hamax_ok[u], 1)

            def h_scale(i, u, last=False):
                dve.wait_ge(hamax_ok[u], 2 * i + 2)
                V.tensor_scalar(c["hclip"](u), hamax[:, u, 0:1], hamax[:, u, 1:2], EPS, ALU.max, ALU.max).then_inc(hclip_ok[u], 1)
                dve.wait_ge(hclip_ok[u], i + 1)
                V.reciprocal(c["hinv"](u), c["hclip"](u)).then_inc(hinv_ok[u], 1)
                dve.wait_ge(hinv_ok[u], i + 1)
                V.tensor_scalar(c["hmul"](u), c["hinv"](u), 127.0, None, ALU.mult).then_inc(hmul_ok[u], 1)
                if not last:
                    y_scale(u)

            def y_scale(u):
                V.tensor_scalar(c["ydq"](u), c["hclip"](u), wdq[:, 2:3], None, ALU.mult).then_inc(ydq_ok[u], 1)

            def hT_copy(i, u, last=False):
                dve.wait_ge(h_mm[u], i + 1)
                dve.wait_ge(w2_mm[u], i)
                if last:
                    V.tensor_copy(hqT[:, u, 4:8, :], XQ_PS).then_inc(hT_b[u], 1)
                V.tensor_copy(hqT[:, u, 8:FC, :], H_PS[1]).then_inc(hT_b[u], 1)

            def quant_last(i, u):
                a = HALVES[1]
                dve.wait_ge(hmul_ok[u], i + 1)
                V.tensor_scalar(hid[:, u, a], hid[:, u, a], c["hmul"](u), MAGIC, ALU.mult, ALU.add).then_inc(last_r, 1)
                dve.wait_ge(last_r, 1)
                dve.wait_ge(h_mm[u], i)
                V.tensor_scalar(hq[:, u, a], hid[:, u, a], -MAGIC, None, ALU.add).then_inc(hq_ok[u], 1)

            def result(i, u, bank=banks[7]):
                dve.wait_ge(w2_mm[u], i + 1)
                dve.wait_ge(ydq_ok[u], i + 1)
                dve.wait_ge(y_out[u], 16 * i)
                V.scalar_tensor_tensor(out=yb[:, u, :], in0=bank[:, :], scalar=c["ydq"](u),
                                       in1=x1[:, bass.ds(2 * i + u, 1), :].rearrange("p a d -> p (a d)"),
                                       op0=ALU.mult, op1=ALU.add).then_inc(y_ok[u], 1)

            def tile(i, u):
                hidden(i, u, (0, 1))
                hT_copy(i + u - 1, 1 - u)
                h_max(i, u, 0)
                hidden(i, u, (2,))
                h_max(i, u, 1)
                h_scale(i, u)
                x_scale(i + 1, u)
                result(i + u - 1, 1 - u)

            def end_pair(i, first=False, last=False):
                hidden(i, 0, (0, 1))
                if not first:
                    hT_copy(i - 1, 1)
                h_max(i, 0, 0)
                hidden(i, 0, (2,), first)
                h_max(i, 0, 1)
                h_scale(i, 0)
                hidden(i, 1, (0,))
                if not last:
                    x_scale(i + 1, 0)
                hidden(i, 1, (1,))
                h_max(i, 1, 0)
                hidden(i, 1, (2,))
                hT_copy(i, 0)
                h_max(i, 1, 1)
                h_scale(i, 1, last)
                if last:
                    quant_last(i, 1)
                else:
                    x_scale(i + 1, 1)
                    result(i, 0)

            pair(0)
            first_half_over(dve)
            V.tensor_scalar(wdq[:, 0:2], wmean[:, 0:2], 1.0 / 127.0, None, ALU.mult).then_inc(wdq_ok, 1)
            V.tensor_scalar(wdq[:, 2:3], wmean[:, 2:3], 1.0 / 127.0, gates[:, 1:2], ALU.mult, ALU.mult).then_inc(wdq_ok, 1)
            dve.wait_ge(wdq_ok, 2)
            moments(0, 2)
            with dve.Fori(1, 3) as i:
                pair(i)
            deviations(0, 2, 1)
            oT_low(3, 1)
            add(3, 0)
            x_scale(0, 0)
            oT_low(4, 0)
            add(3, 1)
            oT_low(4, 1)
            add(4, 0)
            x_scale(0, 1)
            oT_low(5, 0)
            add(4, 1)
            pair(5)
            oT_low(PAIRS - 1, 1)
            moments(2, NT - 2)
            add(PAIRS - 1, 0)
            add(PAIRS - 1, 1)
            moments(NT - 2, NT)
            deviations(2, NT, 2)
            end_pair(0, first=True)
            with dve.Fori(1, PAIRS - 1) as i:
                tile(i, 0)
                tile(i, 1)
            end_pair(PAIRS - 1, last=True)
            result(PAIRS - 2, 1, banks[4])
            hT_copy(PAIRS - 1, 1, last=True)
            dve.wait_ge(y_ok[1], PAIRS - 1)
            y_scale(1)
            result(PAIRS - 1, 0)
            result(PAIRS - 1, 1, banks[0])

        @block.tensor
        def _(pe):
            def products(dst, pairs):
                for n, (a, b) in enumerate(pairs):
                    ins = nc.tensor.matmul(dst, a, b, start=(n == 0), stop=(n == len(pairs) - 1))
                return ins

            def transpose_x(g, u):
                pe.wait_ge(xn_ok[u], g + 1)
                pe.wait_ge(v_lo[u], g)
                for c in range(DC):
                    ins = nc.tensor.transpose(R_BANK[u][:, c * TQ:(c + 1) * TQ], xb[:, u, c * P:(c + 1) * P], ident[0:TQ, 0:TQ])
                ins.then_inc(t_mm[u], 1)

            def qk(g, js):
                for u in range(2):
                    pe.wait_ge(xT_lo[u], g + 1)
                for j in js:
                    pe.wait_ge(pw_lo, min(j + 1, 3))
                    pe.wait_ge(qk_lo[j % 2], 2 * g + j // 2)
                    w = wsp[j // 2]
                    for e in range(2):
                        o = 2 * (j % 2) + e
                        ins = products(Q_BANK[j % 2][:, e * 2 * TQ:(e + 1) * 2 * TQ],
                                       [(w[a][:, c, o * P:(o + 1) * P], xT[b][:, c, :]) for c in range(DC) for a, b in PASSES])
                    ins.then_inc(qk_mm[j % 2], 1)

            def v(g, u):
                pe.wait_ge(pw_lo, len(PW))
                products(R_BANK[u][0:TQ, :], [(xT[a][:, c, u * TQ:(u + 1) * TQ], wsp[2][b][:, c, :])
                                              for c in range(DC) for a, b in PASSES]).then_inc(v_mm[u], 1)

            def scores(g, u):
                for s in qk_lo:
                    pe.wait_ge(s, 2 * g + 2)
                pe.wait_ge(k_split[u], g + 1)
                pe.wait_ge(exp_ok[u], g)
                products(S_BANK[u][0:TQ, 0:KPAD], [(qT[a][:, c, u * TQ:(u + 1) * TQ], kT[b][:, u, c, :])
                                                   for c in range(DC) for a, b in PASSES]).then_inc(s_mm[u], 1)

            def transpose_p(g, u):
                pe.wait_ge(exp_ok[u], g + 1)
                pe.wait_ge(pt_lo[1 - u], g + u)
                for c in range(4):
                    ins = nc.tensor.transpose(PT_BANK[0:CK, c * TQ:(c + 1) * TQ], prob[:, u, c * CK:(c + 1) * CK], ident[0:TQ, 0:TQ])
                ins.then_inc(pt_mm[u], 1)

            def values(g, u):
                pe.wait_ge(pt_lo[u], g + 1)
                pe.wait_ge(v_lo[u], g + 1)
                pe.wait_ge(v_split[u], g + 1)
                pe.wait_ge(o_ok[1 - u], g + u)
                n = [CK, CK, CK, TQ]
                products(AV_BANK[0:TQ, :], [(pT[a][0:n[c], u, c * TQ:(c + 1) * TQ], vv[b][0:n[c], u, c, :])
                                            for c in range(4) for a, b in PASSES]).then_inc(av_mm[u], 1)

            def transpose_o(i, u):
                pe.wait_ge(ot_in[u], 16 * i + 16)
                pe.wait_ge(oT_lo_ok[u], i)
                for c in range(DC):
                    ins = nc.tensor.transpose(banks[u][:, c * P:(c + 1) * P], ot[:, u, c * P:(c + 1) * P], ident[:, :])
                ins.then_inc(ot_mm[u], 1)

            def project(i, u):
                pe.wait_ge(oT_lo_ok[u], i + 1)
                pe.wait_ge(wo_lo_ok, 1)
                pe.wait_ge(x1_ok[u], i)
                products(banks[2 + u][:, :], [(oT[a][:, u, c, :], wo[b][:, c, :])
                                              for c in range(DC) for a, b in PASSES]).then_inc(pr_mm[u], 1)

            def group(g, first=False, scales=False, last=False):
                qk(g, (1, 2, 3))
                v(g, 0)
                scores(g, 0)
                v(g, 1)
                transpose_p(g, 0)
                scores(g, 1)
                if last:
                    transpose_o(0, 0)
                else:
                    transpose_x(g + 1, 0)
                    transpose_x(g + 1, 1)
                if first:
                    pe.wait_ge(gates_ok, 1)
                values(g, 0)
                transpose_p(g, 1)
                if last:
                    transpose_o(0, 1)
                    project(0, 0)
                else:
                    qk(g + 1, (0,))
                if scales:
                    pe.wait_ge(wabs_ok, 1)
                    pe.wait_ge(o_ok[0], g + 1)
                    nc.tensor.matmul(AV_BANK[:, 0:3], ones[:, :], wabs3[:, :], start=True, stop=True).then_inc(sum_mm, 1)
                    pe.wait_ge(wmean_ok, 1)
                values(g, 1)

            pe.wait_ge(consts, 11)
            transpose_x(0, 0)
            transpose_x(0, 1)
            pe.wait_ge(g_in, 32)
            nc.tensor.matmul(AV_BANK[:, 0:2], ones[0:1, :], gin[0:1, :], start=True, stop=True).then_inc(sum_mm, 1)
            qk(0, (0,))
            group(0, first=True)
            with pe.Fori(1, 3) as g:
                group(g)
            group(3, scales=True)
            with pe.Fori(4, 7) as g:
                group(g)
            group(7, last=True)

            def transpose_xq(i, u):
                pe.wait_ge(xq_ok[u], i + 1)
                pe.wait_ge(xqT_ok[1 - u], i + u)
                for c in range(DC):
                    ins = nc.tensor.transpose(XQ_PS[:, c, :], xq[:, u, c * P:(c + 1) * P], identb[:, :])
                ins.then_inc(xq_mm[u], 1)

            def pair(i):
                transpose_o(i, 1)
                project(i, 0)
                transpose_o(i + 1, 0)
                project(i, 1)

            transpose_o(1, 0)
            project(0, 1)
            with pe.Fori(1, PAIRS - 1) as i:
                pair(i)
            transpose_o(PAIRS - 1, 1)
            project(PAIRS - 1, 0)
            transpose_xq(0, 0)
            project(PAIRS - 1, 1)
            transpose_xq(0, 1)

            def up(i, u, j, first=False, second=False):
                a, n = HCH[j]
                k, turn = bank_turn(u, j)
                pair = SPARE if first and j == 2 else (banks[k], banks[2 + k])
                pe.wait_ge(xqT_ok[u], i + 1)
                if first and j < 2:
                    pe.wait_ge(x1_ok[k], PAIRS)
                elif not first:
                    pe.wait_ge(h_ok[k], 1 if second else 3 * i + turn)
                products(pair[0][:, 0:n], [(xqT[:, u, c, :], WQ[:, c, a:a + n]) for c in range(DC)])
                products(pair[1][:, 0:n], [(xqT[:, u, c, :], WQ[:, 4 + c, a:a + n])
                                           for c in range(DC)]).then_inc(ab_mm[k], 1)

            def transpose_h(i, u, last=False):
                if last:
                    pe.wait_ge(y_ok[u], i)
                pe.wait_ge(hq_ok[u], 2 * i + 2)
                pe.wait_ge(hT_a[1 - u], i + u)
                pe.wait_ge(hT_b[1 - u], i + u)
                for c in range(FC):
                    to = XQ_PS[:, c - 4, :] if last and 4 <= c < 8 else H_PS[c // 8][:, c % 8, :]
                    ins = nc.tensor.transpose(to, hq[:, u, c * P:(c + 1) * P], identb[:, :])
                ins.then_inc(h_mm[u], 1)

            def down(i, u):
                pe.wait_ge(hT_a[u], i + 1)
                pe.wait_ge(hT_b[u], i + 1)
                pe.wait_ge(y_ok[1 - u], i + u)
                products(banks[7][:, :], [(hqT[:, u, c, :], w2q[:, c, :]) for c in range(FC)]).then_inc(w2_mm[u], 1)

            def down_part(i, u, bank, chunks):
                for c in chunks:
                    ins = nc.tensor.matmul(bank[:, :], hqT[:, u, c, :], w2q[:, c, :], start=(c == 0), stop=(c == FC - 1))
                if c == FC - 1:
                    ins.then_inc(w2_mm[u], 1)

            def down_late(i, u):
                pe.wait_ge(hT_a[u], i + 1)
                pe.wait_ge(hT_b[u], i + 1)
                pe.wait_ge(xqT_ok[u], PAIRS)
                down_part(i, u, banks[4], range(FC))

            def down_last(i, u):
                pe.wait_ge(hT_a[u], i + 1)
                for c in range(FC):
                    if c == 4:
                        pe.wait_ge(hT_b[u], i + 1)
                    if c == 8:
                        pe.wait_ge(hT_b[u], i + 2)
                    down_part(i, u, banks[0], (c,))

            def tile(i, u):
                up(i, u, 0)
                up(i, u, 1)
                transpose_h(i + u - 1, 1 - u)
                up(i, u, 2)
                transpose_xq(i + u, 1 - u)
                down(i + u - 1, 1 - u)

            def end_pair(i, first=False, last=False):
                up(i, 0, 0, first)
                up(i, 0, 1, first)
                if not first:
                    transpose_h(i - 1, 1)
                    transpose_xq(i, 1)
                up(i, 0, 2, first)
                up(i, 1, 0)
                up(i, 1, 1, second=first)
                up(i, 1, 2)
                transpose_h(i, 0)
                if not last:
                    transpose_xq(i + 1, 0)
                    down(i, 0)

            end_pair(0, first=True)
            with pe.Fori(1, PAIRS - 1) as i:
                tile(i, 0)
                tile(i, 1)
            end_pair(PAIRS - 1, last=True)
            down_late(PAIRS - 2, 1)
            pe.wait_ge(hT_a[0], PAIRS)
            pe.wait_ge(hT_b[0], PAIRS)
            pe.wait_ge(y_ok[0], PAIRS - 1)
            down_part(PAIRS - 1, 0, banks[7], range(6))
            transpose_h(PAIRS - 1, 1, last=True)
            down_part(PAIRS - 1, 0, banks[7], range(6, FC))
            for s in h_ok:
                pe.wait_ge(s, 3 * PAIRS)
            down_last(PAIRS - 1, 1)


def kernel(x, ctx_2048, mask_BxSx4224_bf0, g_xattn, g_ffn, L0_xattn_wq, L0_xattn_wk, L0_xattn_wv, L0_xattn_wo,
           L0_ffn_w1, L0_ffn_w2, L0_ffn_w3):
    import concourse.bacc as bacc
    from concourse.bass_utils import run_bass_kernel_spmd

    def chunks(w):
        w = np.asarray(w)
        return np.ascontiguousarray(w.T.reshape(w.shape[1] // P, P, w.shape[0]).transpose(1, 0, 2))

    c = np.asarray(ctx_2048)
    keys = c.reshape(B, CK, 3, DC, P).transpose(0, 4, 3, 2, 1).reshape(B, P, DC, KC)
    ffn = np.concatenate([chunks(L0_ffn_w1).transpose(1, 0, 2), chunks(L0_ffn_w3).transpose(1, 0, 2),
                          chunks(L0_ffn_w2).reshape(P, 4, F).transpose(1, 0, 2)])
    arrays = {
        "x": np.ascontiguousarray(np.asarray(x).reshape(TOK, D)),
        "ctxT": np.ascontiguousarray(keys),
        "ctx": np.ascontiguousarray(c.reshape(B, CK, 3, D)),
        "g_xattn": np.ascontiguousarray(g_xattn),
        "g_ffn": np.ascontiguousarray(g_ffn),
        "wqT": chunks(L0_xattn_wq), "wkT": chunks(L0_xattn_wk), "wvT": chunks(L0_xattn_wv), "woT": chunks(L0_xattn_wo),
        "wffn": np.ascontiguousarray(ffn),
    }
    nc = bacc.Bacc("TRN2", target_bir_lowering=False, num_devices=1)
    ins = [nc.dram_tensor(n, a.shape, mybir.dt.from_np(a.dtype), kind="ExternalInput").ap() for n, a in arrays.items()]
    out = nc.dram_tensor("out", (TOK, D), mybir.dt.float32, kind="ExternalOutput").ap()
    o_dram = nc.dram_tensor("o_dram", (TOK, D), mybir.dt.float32, kind="Internal").ap()
    flamingo_kernel(nc, *ins, out, o_dram)
    r = run_bass_kernel_spmd(nc, [arrays], core_ids=[0])
    return np.asarray(r.results[0]["out"]).reshape(B, TQ, D)
```
